# Optimizing a Trainium2 kernel written in Bass

```python
import numpy as np
import jax
import jax.numpy as jnp

def _softmax(x, axis=-1):
    return jax.nn.softmax(x, axis=axis)

def _gelu(x):
    return jax.nn.gelu(x, approximate=True)

def _silu(x):
    return jax.nn.silu(x)

def _sigmoid(x):
    return jax.nn.sigmoid(x)

def _layernorm(x, axis=-1, eps=1e-05):
    m = jnp.mean(x, axis=axis, keepdims=True)
    v = jnp.var(x, axis=axis, keepdims=True)
    return (x - m) / jnp.sqrt(v + eps)

def _scatter_add(tgt, idx, src, axis=0):
    return tgt.at[idx].add(src)

def _segment_sum(src, seg, n):
    return jax.ops.segment_sum(src, seg, n)
kernel_name = 'mk_gnn_resnorm_d2_gnn_r8_27d21a'

def setup_inputs(seed: int=0):
    np.random.seed(seed)
    _w = jnp.asarray

    def _rec_inputs():
        import jax
        import jax.numpy as jnp
        _gk = jax.random.key(seed)
        x = -0.000202 + 1 * jax.random.normal(jax.random.fold_in(_gk, 1), (6250, 128), jnp.float32)
        _s = jax.random.randint(jax.random.fold_in(_gk, 2), (50000,), 0, 6250, jnp.int32)
        _d = jax.random.randint(jax.random.fold_in(_gk, 3), (50000,), 0, 6250, jnp.int32)
        _loop = jnp.arange(6250, dtype=jnp.int32)
        src = jnp.concatenate([_s, _d, _loop])
        dst = jnp.concatenate([_d, _s, _loop])
        _o = jnp.argsort(dst, stable=True)
        src = src[_o]
        dst = dst[_o]
        edge_type_8 = jax.random.randint(jax.random.fold_in(_gk, 12), (106250,), 0, 8, jnp.int32)
        edge_weight1 = jax.random.uniform(jax.random.fold_in(_gk, 13), (106250, 1), jnp.float32, 0.0, 1)
        return (x, src, dst, edge_type_8, edge_weight1)
    x, src, dst, edge_type_8, edge_weight1 = _rec_inputs()

    def _L0_gnn_setup():
        import jax, jax.numpy as jnp
        import numpy as np
        N = 6250
        E = 100000
        C_IN = 128
        C_HID = 128
        key = jax.random.key(seed)
        ks = jax.random.split(key, 8)
        node_embed = jax.random.normal(ks[0], (N, C_IN), dtype=jnp.float32)
        edge_dist = jax.random.uniform(ks[1], (E, 1), dtype=jnp.float32)
        edge_index = jax.random.randint(ks[2], (2, E), 0, N, dtype=jnp.int64)
        msg_in = 2 * C_IN + 1
        W_res = jax.random.uniform(ks[3], (C_IN, C_HID), dtype=jnp.float32, minval=-1, maxval=1) / np.sqrt(C_IN)
        W_msg = jax.random.uniform(ks[4], (msg_in, C_HID), dtype=jnp.float32, minval=-1, maxval=1) / np.sqrt(msg_in)
        b_msg = jnp.zeros((C_HID,), dtype=jnp.float32)
        W_upd = jax.random.uniform(ks[5], (C_IN + C_HID, C_HID), dtype=jnp.float32, minval=-1, maxval=1) / np.sqrt(C_IN + C_HID)
        b_upd = jnp.zeros((C_HID,), dtype=jnp.float32)
        return {'node_embed': node_embed, 'edge_dist': edge_dist, 'edge_index': edge_index, 'W_res': W_res, 'W_msg': W_msg, 'b_msg': b_msg, 'W_upd': W_upd, 'b_upd': b_upd}
    _L0_gnn_all = _L0_gnn_setup()
    _L0_gnn_in = {k: v for k, v in _L0_gnn_all.items() if k in ('W_res', 'W_msg', 'b_msg', 'W_upd', 'b_upd')}
    del _L0_gnn_all

    def _L1_gnn_setup():
        import jax, jax.numpy as jnp
        import numpy as np
        N_REL = 8
        EPS = 1e-05

        def _rgcn_bn_mish(x, W, root, bias, gamma, beta, edge_index, edge_type):
            N = x.shape[0]
            src, dst = (edge_index[0], edge_index[1])
            h = jnp.einsum('ni,rio->rno', x, W)
            seg = edge_type * N + dst
            counts = jax.ops.segment_sum(jnp.ones(edge_type.shape, dtype=x.dtype), seg, num_segments=N_REL * N).reshape(N_REL, N)
            counts = jnp.maximum(counts, 1.0)
            msgs = h[edge_type, src] / counts[edge_type, dst][:, None]
            agg = jax.ops.segment_sum(msgs, dst, num_segments=N)
            out = agg + x @ root + bias
            mu = jnp.mean(out, axis=0)
            var = jnp.var(out, axis=0)
            out = (out - mu) * jax.lax.rsqrt(var + EPS) * gamma + beta
            return out * jnp.tanh(jax.nn.softplus(out))
        key = jax.random.key(seed)
        k1, k2, k3, k4, k5 = jax.random.split(key, 5)
        N, E, D_IN, D_OUT = (12500, 75000, 128, 128)
        x = jax.random.normal(k1, (N, D_IN), dtype=jnp.float32)
        edge_index = jax.random.randint(k2, (2, E), 0, N, dtype=jnp.int64)
        edge_type = jax.random.randint(k3, (E,), 0, N_REL, dtype=jnp.int64)
        W = jax.random.normal(k4, (N_REL, D_IN, D_OUT), dtype=jnp.float32) * 0.05
        root = jax.random.normal(k5, (D_IN, D_OUT), dtype=jnp.float32) * 0.05
        bias = jnp.zeros((D_OUT,), dtype=jnp.float32)
        gamma = jnp.ones((D_OUT,), dtype=jnp.float32)
        beta = jnp.zeros((D_OUT,), dtype=jnp.float32)
        return {'x': x, 'edge_index': edge_index, 'edge_type': edge_type, 'W': W, 'root': root, 'bias': bias, 'gamma': gamma, 'beta': beta}
    _L1_gnn_all = _L1_gnn_setup()
    _L1_gnn_in = {k: v for k, v in _L1_gnn_all.items() if k in ('W', 'root', 'bias', 'gamma', 'beta')}
    del _L1_gnn_all
    return {'x': x, 'src': src, 'dst': dst, 'edge_type_8': edge_type_8, 'edge_weight1': edge_weight1, 'L0_gnn_W_res': _L0_gnn_in['W_res'], 'L0_gnn_W_msg': _L0_gnn_in['W_msg'], 'L0_gnn_b_msg': _L0_gnn_in['b_msg'], 'L0_gnn_W_upd': _L0_gnn_in['W_upd'], 'L0_gnn_b_upd': _L0_gnn_in['b_upd'], 'L1_gnn_W': _L1_gnn_in['W'], 'L1_gnn_root': _L1_gnn_in['root'], 'L1_gnn_bias': _L1_gnn_in['bias'], 'L1_gnn_gamma': _L1_gnn_in['gamma'], 'L1_gnn_beta': _L1_gnn_in['beta']}

def reference(x, src, dst, edge_type_8, edge_weight1, L0_gnn_W_res, L0_gnn_W_msg, L0_gnn_b_msg, L0_gnn_W_upd, L0_gnn_b_upd, L1_gnn_W, L1_gnn_root, L1_gnn_bias, L1_gnn_gamma, L1_gnn_beta):
    import jax
    import jax.numpy as jnp

    def _L0_gnn_ref(node_embed, edge_dist, edge_index, W_res, W_msg, b_msg, W_upd, b_upd):
        import jax, jax.numpy as jnp
        import numpy as np
        N = 6250
        E = 100000
        C_IN = 128
        C_HID = 128
        row, col = (edge_index[0], edge_index[1])
        msg_repr = jnp.concatenate((node_embed[row], node_embed[col], edge_dist), axis=-1)
        node_messages = jax.nn.relu(msg_repr @ W_msg + b_msg)
        aggr = jax.ops.segment_sum(node_messages, col, num_segments=node_embed.shape[0])
        upd_in = jnp.concatenate((node_embed, aggr), axis=-1)
        new_node_embed = node_embed @ W_res + jax.nn.relu(upd_in @ W_upd + b_upd)
        return new_node_embed

    def _L1_gnn_ref(x, edge_index, edge_type, W, root, bias, gamma, beta):
        import jax, jax.numpy as jnp
        import numpy as np
        N_REL = 8
        EPS = 1e-05

        def _rgcn_bn_mish(x, W, root, bias, gamma, beta, edge_index, edge_type):
            N = x.shape[0]
            src, dst = (edge_index[0], edge_index[1])
            h = jnp.einsum('ni,rio->rno', x, W)
            seg = edge_type * N + dst
            counts = jax.ops.segment_sum(jnp.ones(edge_type.shape, dtype=x.dtype), seg, num_segments=N_REL * N).reshape(N_REL, N)
            counts = jnp.maximum(counts, 1.0)
            msgs = h[edge_type, src] / counts[edge_type, dst][:, None]
            agg = jax.ops.segment_sum(msgs, dst, num_segments=N)
            out = agg + x @ root + bias
            mu = jnp.mean(out, axis=0)
            var = jnp.var(out, axis=0)
            out = (out - mu) * jax.lax.rsqrt(var + EPS) * gamma + beta
            return out * jnp.tanh(jax.nn.softplus(out))
        return _rgcn_bn_mish(x, W, root, bias, gamma, beta, edge_index, edge_type)
    edge_index = jnp.stack([src, dst])
    x = _layernorm(x + _L0_gnn_ref(x, edge_weight1, edge_index, L0_gnn_W_res, L0_gnn_W_msg, L0_gnn_b_msg, L0_gnn_W_upd, L0_gnn_b_upd), axis=-1)
    x = _layernorm(x + _L1_gnn_ref(x, edge_index, edge_type_8, L1_gnn_W, L1_gnn_root, L1_gnn_bias, L1_gnn_gamma, L1_gnn_beta), axis=-1)
    return x

_drawn_inputs = setup_inputs


def setup_inputs(seed=0):
    import zlib

    import numpy as np

    out = dict(_drawn_inputs(seed))
    spreads = {'L0_gnn_b_msg': (0.0, 0.1),
     'L0_gnn_b_upd': (0.0, 0.1),
     'L1_gnn_bias': (0.0, 0.8),
     'L1_gnn_gamma': (1.0, 0.2),
     'L1_gnn_beta': (0.0, 0.1)}
    factors = {'edge_weight1': 8.0}
    for name, (base, spread) in spreads.items():
        noise = np.random.default_rng([zlib.crc32(name.encode()), seed]).standard_normal(out[name].shape)
        drawn = base * np.exp(spread * noise) if base else spread * noise
        out[name] = jnp.asarray(drawn.astype(out[name].dtype))
    for name, factor in factors.items():
        out[name] = (out[name] * factor).astype(out[name].dtype)
    return out
```

```python
from contextlib import ExitStack

import concourse.bass as bass
from concourse import mybir

ALU = mybir.AluOpType
ACT = mybir.ActivationFunctionType
AX = mybir.AxisListType
F32 = mybir.dt.float32
BF16 = mybir.dt.bfloat16
I32 = mybir.dt.int32

P = 128
QT = 4
SLOTS = 8
HALF = SLOTS // 2
EPS = 1e-5
FAR = 1 << 20
EXP_CAP = 20.0


class Stage:

    def __init__(self, sem, credit=2):
        self.sem, self.credit = sem, credit

    def after(self, n):
        return n + (1 + self.credit)


def bass_gnn(nc, x, src, dst, edge_type, edge_weight, w_res, w_msg, b_msg, w_upd, b_upd,
             w_rel, w_root, b_rel, gamma, beta, out):
    N, C = x.shape
    E = src.shape[0]
    R = w_rel.shape[0]
    assert C == P
    BLOCKS = -(-N // P)
    LAST = N - (BLOCKS - 1) * P
    QUADS = -(-E // (P * QT * SLOTS)) * SLOTS
    TILES = QUADS * QT
    ITERS = QUADS // SLOTS
    CH = -(-TILES // P)
    COLS = CH * P
    GB = 4
    GROUPS = BLOCKS // GB
    assert BLOCKS % GB == 1 and GROUPS % 2 == 0 and (QUADS - 1) * QT * P < E
    FULL = E // P
    NW = (BLOCKS + 1) * P
    PASSES = 1 + BLOCKS
    BODY_T = SLOTS * QT
    STAGE_T = HALF * QT
    SC = max(d for d in range(1, 513) if N % d == 0)
    NST = N // SC
    UPD_STEPS = 14

    src_rows = nc.dram_tensor("src_rows", (BLOCKS * P, C), F32).ap()
    rel_rows = nc.dram_tensor("rel_rows", (BLOCKS * P * R, C), F32).ap()

    ctx = ExitStack()
    with ctx:
        def sb(name, shape, dt=F32):
            return ctx.enter_context(nc.sbuf_tensor(name, shape, dt))

        def sem(name):
            return ctx.enter_context(nc.semaphore(name))

        bank = [ctx.enter_context(nc.psum_tensor(f"bank{i}", [P, 512], F32)) for i in range(8)]

        ident = sb("ident", [P, P])
        node_iota = sb("node_iota", [P, P])
        ones = sb("ones", [P, P])
        w_ab = sb("w_ab", [P, 2, C])
        w_dist = sb("w_dist", [P, C])
        w_self = sb("w_self", [P, C])
        w_up = sb("w_up", [P, 2, C])
        w_r = sb("w_r", [P, R, C])
        w_ro = sb("w_ro", [P, C])
        bmsg = sb("bmsg", [P, C])
        bupd = sb("bupd", [P, C])
        chan = sb("chan", [P, 3])
        onehot = sb("onehot", [P, 4, QT, P])
        onehot_mem = onehot[:, :, :, :].rearrange("p b j c -> p (b j c)")
        src_f = onehot_mem[:, 0:COLS]
        dst_f = onehot_mem[:, COLS:2 * COLS]
        type_f = sb("type_f", [P, COLS])
        dist = sb("dist", [P, COLS])
        idx = [sb(f"idx{k}", [P, TILES + BODY_T], I32) for k in range(2)]
        idx_stage = sb("idx_stage", [P, 2, STAGE_T], I32)
        rel0 = sb("rel0", [P, TILES])
        far0 = sb("far0", [P, TILES])
        rel = sb("rel", [P, TILES])
        inside = src_f[:, 0:TILES]
        moved = sb("moved", [P, PASSES])
        outside = rel
        n_far = sb("n_far", [P, 1])
        passes_f = sb("passes_f", [1, 2])
        passes_i = sb("passes_i", [1, 1], I32)
        win_tab = sb("win_tab", [1, 2 * QUADS + BLOCKS], I32)
        pass_tab = sb("pass_tab", [1, 2, PASSES], I32)
        win_mem = sb("win_mem", [P, BLOCKS * 3 * C])
        tgt_win = win_mem[:, :].bitcast(BF16).rearrange("p (q h k c) -> p q h k c", h=2, k=3, c=C)
        x1 = win_mem[:, 0:BLOCKS * C].rearrange("p (q c) -> p q c", c=C)
        inv_win = sb("inv_win", [P, BLOCKS, 2, 3, R], BF16)
        agg = sb("agg", [P, NW])
        raw = agg[:, 0:3 * COLS].bitcast(I32).rearrange("p (k c e) -> p k c e", k=3, e=P)
        raw_w = agg[:, 3 * COLS:4 * COLS].rearrange("p (c e) -> p c e", e=P)
        rawf = agg[:, 4 * COLS:7 * COLS].rearrange("p (k c e) -> p k c e", k=3, e=P)
        cnt = sb("cnt", [R, NW])
        rows = sb("rows", [P, SLOTS, QT, C])
        onehot_t = sb("onehot_t", [P, 2, QT, P], BF16)
        types = sb("types", [P, 4, QT, 3, R])
        pre = sb("pre", [P, 2, QT, C])
        msg = sb("msg", [P, 2, QT, C])
        picked = sb("picked", [P, QT, 3 * R])
        edge_w = sb("edge_w", [P, 2, QT])
        first_i = rows[0:1, 6, :, :].rearrange("p a b -> p (a b)")[:, 0:QUADS].bitcast(I32)
        win_f = rows[0:1, 7, :, :].rearrange("p a b -> p (a b)")[:, 0:QUADS]
        xs = rows[:, 0:2, :, :]
        xT = rows[:, 2:4, :, :]
        a_out = rows[:, 4:6, :, :]
        hs = rows[:, 4:8, :, :].rearrange("p (b a) t c -> p b (a t c)", b=2)
        bsum = msg[:, 0, :, :]
        bres = msg[:, 1, :, :]
        part_mem = sb("part_mem", [P, GB * 3 * C // 2])
        b3 = part_mem[:, :].bitcast(BF16).rearrange("p (k h c) -> p k h c", k=GB, h=3)
        x1s = onehot[:, 0:2, :, :]
        aT = pre
        x1T = part_mem[:, 0:GB * P].rearrange("p (k c) -> p k c", k=GB)
        y2 = msg[:, 0, :, :]
        y = msg[:, 1, :, :]
        st6 = sb("st6", [P, GB, 6])
        mv = sb("mv", [P, GB, 2])
        vare = sb("vare", [P, GB])
        sd = sb("sd", [P, GB])
        rstd = sb("rstd", [P, GB])
        cs = [onehot_mem[0:R, 2 * QT * P:2 * QT * P + GB * P + P // 2], rel[0:R, 0:GB * P + P // 2]]
        inv = sb("inv", [P, 2 * GB, R])
        inv_r = sb("inv_r", [P, 2 * GB, R])
        inv3 = sb("inv3", [P, 2 * GB, 3, R], BF16)
        zb, ez, cap = pre, onehot[:, 0:2, :, :], msg
        bst = sb("bst", [P, NST, 6])
        bmv = sb("bmv", [P, 2])
        baff = sb("baff", [P, 6])
        mvall = sb("mvall", [P, BLOCKS, 2])
        sdall = far0[:, 0:3 * BLOCKS].rearrange("p (k q) -> p k q", k=3)

        s_w, s_const, s_pad, s_edges = sem("weights_loaded"), sem("constants_set"), sem("edge_padding_set"), sem("edges_loaded")
        s_cast, s_etr, s_ecp = sem("edges_cast"), sem("edges_transposed"), sem("edges_copied")
        s_base, s_baseb = sem("window_starts_ready"), sem("window_starts_spread")
        s_nfar, s_nfars, s_tab = sem("far_edges_counted"), sem("far_edges_summed"), sem("tables_ready")
        s_clear = sem("sums_cleared")
        s_tail = sem("tail_rows_zeroed")
        gm = sem("waits_taken")
        c_edge, c_prep, c_upd, c_fin, c_nrm, c_act = (sem(f"chain_{n}") for n in ("edges", "prepare", "update", "final", "norm", "act"))
        xl = [sem(f"x_loaded{i}") for i in range(2)]
        aw = [sem(f"source_part_written{i}") for i in range(2)]
        xtr, xtc, abm, ac, bc = (Stage(sem(n)) for n in (
            "x_transposed", "x_transpose_copied", "parts_multiplied", "source_part_copied", "target_part_read"))
        s_odd = sem("odd_windows_ready")
        L = [dict(
            staged=sem(f"indices_staged{k}"),
            gathered=[sem(f"gathered{k}_{s}") for s in range(SLOTS)],
            issued=sem(f"quads_issued{k}"),
            targets=sem(f"targets_ready{k}"),
            used=Stage(sem(f"rows_used{k}"), SLOTS),
            **{n: Stage(sem(f"{n}{k}")) for n in (
                "onehot_ready", "onehot_turned", "turned_copied", "looked_up", "lookup_used",
                "picked_ready", "messages_ready", "window_added", "counts_added")},
            scattered=Stage(sem(f"scattered{k}"), 4),
        ) for k in range(2)]
        l_done = [sem(f"layer_summed{k}") for k in range(2)]
        ul = [sem(f"update_x_loaded{i}") for i in range(2)]
        u_hw = [sem(f"relation_rows_written{i}") for i in range(2)]
        (u_st, u_cs, u_tr, u_tc, u_mm, u_y, u_var, u_sd, u_x1, u_x1k, u_t1, u_t1c, u_root, u_rootc, u_h0, u_h1, u_hc0, u_hc1,
         u_ct, u_iv) = (Stage(sem(n)) for n in (
            "sums_staged", "counts_staged", "update_x_transposed", "update_x_copied", "update_multiplied", "update_y_ready",
            "update_variance_ready", "update_deviation_ready", "x1_ready", "x1_kept", "x1_transposed", "x1_transpose_copied",
            "root_multiplied", "root_added", "relations_low_multiplied", "relations_high_multiplied",
            "relations_low_copied", "relations_high_copied", "counts_transposed", "inverse_started"))
        s_bv, s_bsd, s_aff = sem("batch_variance_ready"), sem("batch_deviation_ready"), sem("batch_affine_ready")
        f_z, f_cap, f_exp, f_m, f_tr, f_y = (Stage(sem(n)) for n in (
            "final_z_ready", "final_capped", "final_exp_ready", "final_mish_ready", "final_transposed", "final_y_read"))
        s_fv, s_fsd = sem("final_variances_ready"), sem("final_deviations_ready")
        f_n = Stage(sem("final_normalised"))
        f_o = [sem(f"final_written{i}") for i in range(2)]

        x_groups = x[0:GROUPS * GB * P, :].rearrange("(q p) c -> p q c", p=P)
        src_groups = src_rows[0:GROUPS * GB * P, :].rearrange("(q p) c -> p q c", p=P)
        out_groups = out[0:GROUPS * GB * P, :].rearrange("(q p) c -> p q c", p=P)
        rel_blocks = rel_rows.rearrange("(q p r) c -> p q (r c)", p=P, r=R)

        class Group:

            def __init__(self, pair, b):
                self.pair, self.b, self.g = pair + b // 2, b % 2, pair * 2 + b
                self.first = isinstance(self.g, int) and self.g < 2
                self.tail = isinstance(self.g, int) and self.g == GROUPS
                self.nb = 1 if self.tail else GB

        def groups(eng, step):
            step(Group(0, 0))
            step(Group(0, 1))
            with eng.Fori(1, GROUPS // 2) as i:
                step(Group(i, 0))
                step(Group(i, 1))
            step(Group(GROUPS // 2, 0))

        def skewed(eng, a, b):
            a(Group(0, 0))
            for k in range(2):
                a(Group(0, k + 1))
                b(Group(0, k))
            with eng.Fori(1, GROUPS // 2 - 1) as i:
                for k in range(2):
                    a(Group(i, k + 1))
                    b(Group(i, k))
            for k in range(2):
                a(Group(GROUPS // 2 - 1, k + 1))
                b(Group(GROUPS // 2 - 1, k))
            b(Group(GROUPS // 2, 0))

        class Chain:

            def __init__(self, eng, s, base=0):
                self.eng, self.s, self.base, self.n = eng, s, base, 0

            def step(self, ins):
                self.n += 1
                ins.then_inc(self.s, 1)
                self.eng.wait_ge(self.s, self.base + self.n)

        def over(v, nb):
            return v[:, :].unsqueeze(1).broadcast_to([P, nb, C])

        def start_credits(eng, *stages):
            for s in stages:
                eng.sem_inc(s.sem, s.credit)

        def pass_values(eng, p):
            at = eng.value_load(pass_tab[0:1, 0, bass.ds(p, 1)], min_val=0, max_val=QUADS + BLOCKS - 1)
            step = eng.value_load(pass_tab[0:1, 1, bass.ds(p, 1)], min_val=0, max_val=1)
            return at, step

        def window_of(eng, i, s, at, step):
            return eng.value_load(win_tab[0:1, bass.ds(at + (i * SLOTS + s) * step, 1)], min_val=0, max_val=2 * BLOCKS - 1)

        block = ctx.enter_context(nc.Block())

        @block.sync
        def _(sp):
            first = (FULL // P) * P * P
            full = (FULL % P) * P
            sp.wait_ge(s_pad, 4)
            for k, e in enumerate((src, dst, edge_type, edge_weight)):
                d = raw[:, k, :, :] if k < 3 else raw_w
                e = e if k < 3 else e.rearrange("e a -> (e a)")
                sp.dma_start(d[:, 0:FULL // P, :], e[0:first].rearrange("(c p e) -> p c e", p=P, e=P)).then_inc(s_edges, 16)
                sp.dma_start(d[0:FULL % P, FULL // P, :],
                             e[first:first + full].rearrange("(p e) -> p e", e=P)).then_inc(s_edges, 16)
                sp.dma_start(d[FULL % P:FULL % P + 1, FULL // P, 0:E - FULL * P],
                             e[FULL * P:E].rearrange("(p e) -> p e", p=1)).then_inc(s_edges, 16)
            sp.dma_start(w_ab[:, :, :], w_msg[0:2 * C, :].rearrange("(k p) c -> p k c", p=P)).then_inc(s_w, 16)
            sp.dma_start(bmsg[:, :], b_msg.partition_broadcast(P)).then_inc(s_w, 16)
            sp.dma_start(w_dist[:, :], w_msg[2 * C, :].partition_broadcast(P)).then_inc(s_w, 16)
            sp.dma_start(w_self[:, :], w_res).then_inc(s_w, 16)
            sp.dma_start(w_up[:, :, :], w_upd.rearrange("(k p) c -> p k c", p=P)).then_inc(s_w, 16)
            sp.dma_start(bupd[:, :], b_upd.partition_broadcast(P)).then_inc(s_w, 16)
            sp.dma_start(w_r[:, :, :], w_rel.rearrange("r p c -> p r c")).then_inc(s_w, 16)
            sp.dma_start(w_ro[:, :], w_root).then_inc(s_w, 16)
            for k, v in enumerate((b_rel, gamma, beta)):
                sp.dma_start(chan[:, k:k + 1], v.rearrange("(p a) -> p a", a=1)).then_inc(s_w, 16)

            def load_x(G, loaded, used, tails):
                if G.tail:
                    sp.wait_ge(s_tail, tails)
                    sp.dma_start(xs[0:LAST, 0, 0, :], x[GROUPS * GB * P:N, :]).then_inc(loaded[0], 16)
                else:
                    sp.wait_ge(used.sem, used.after(G.g - 2))
                    sp.dma_start(xs[:, G.b, :, :], x_groups[:, bass.ds(G.g * GB, GB), :]).then_inc(loaded[G.b], 16)

            groups(sp, lambda G: load_x(G, xl, xtr, 1))
            sp.wait_ge(s_clear, 3)
            sp.wait_ge(c_prep, (GROUPS + 1) * 6)
            sp.dma_start(tgt_win[0:P // 2, :, 1, :, :], tgt_win[P // 2:P, :, 0, :, :]).then_inc(s_odd, 16)
            sp.dma_start(tgt_win[P // 2:P, 0:BLOCKS - 1, 1, :, :], tgt_win[0:P // 2, 1:BLOCKS, 0, :, :]).then_inc(s_odd, 16)

            sp.wait_ge(l_done[0], 1)
            groups(sp, lambda G: load_x(G, ul, u_y, 2))

            def store(G):
                sp.wait_ge(f_n.sem, f_n.after(G.g))
                if G.tail:
                    sp.dma_start(out[GROUPS * GB * P:N, :], xs[0:LAST, 0, 0, :]).then_inc(f_o[0], 16)
                else:
                    sp.dma_start(out_groups[:, bass.ds(G.g * GB, GB), :], xs[:, G.b, :, :]).then_inc(f_o[G.b], 16)
            groups(sp, store)
            sp.wait_ge(f_o[0], 16 * (GROUPS // 2 + 1))
            sp.wait_ge(f_o[1], 16 * (GROUPS // 2))

        @block.gpsimd
        def _(pool):
            nc.gpsimd.memset(ident[:, :], 0.0).then_inc(s_const, 1)
            pool.wait_ge(s_const, 1)
            nc.gpsimd.affine_select(out=ident[:, :], in_=ident[:, :], compare_op=ALU.not_equal, fill=1.0,
                                    base=0, pattern=[[-1, P]], channel_multiplier=1).then_inc(s_const, 1)
            nc.gpsimd.iota(node_iota[:, :], [[1, P]], base=0, channel_multiplier=0,
                           allow_small_or_imprecise_dtypes=True).then_inc(s_const, 1)
            nc.gpsimd.memset(ones[:, :], 1.0).then_inc(s_const, 1)
            nc.gpsimd.iota(pass_tab[0:1, 0, 1:PASSES], [[1, BLOCKS]], base=QUADS, channel_multiplier=0).then_inc(s_const, 1)
            nc.gpsimd.memset(pass_tab[0:1, 0, 0:1], 0).then_inc(s_const, 1)
            nc.gpsimd.memset(pass_tab[0:1, 1, 1:PASSES], 0).then_inc(s_const, 1)
            nc.gpsimd.memset(pass_tab[0:1, 1, 0:1], 1).then_inc(s_const, 1)
            nc.gpsimd.iota(moved[:, :], [[P, PASSES]], base=0, channel_multiplier=0,
                           allow_small_or_imprecise_dtypes=True).then_inc(s_const, 1)
            nc.gpsimd.iota(win_tab[0:1, QUADS:QUADS + BLOCKS], [[2, BLOCKS]], base=0, channel_multiplier=0).then_inc(s_const, 1)
            nc.gpsimd.memset(cnt[:, :], 0.0).then_inc(s_clear, 1)
            pool.wait_ge(s_etr, 4)
            nc.gpsimd.memset(agg[:, :], 0.0).then_inc(s_clear, 1)

            def write_source_part(G):
                pool.wait_ge(ac.sem, ac.after(G.g))
                pool.sem_inc(gm, 1)
                if G.tail:
                    pool.dma_start(src_rows[GROUPS * GB * P:, :], a_out[:, 0, 0, :]).then_inc(aw[0], 16)
                else:
                    pool.dma_start(src_groups[:, bass.ds(G.g * GB, GB), :], a_out[:, G.b, :, :]).then_inc(aw[G.b], 16)
            groups(pool, write_source_part)

            def gather(k, table):
                l = L[k]
                used = l["used"]
                passes = pool.value_load(passes_i[0:1, 0:1], min_val=1, max_val=PASSES)
                with pool.Fori(0, passes) as p:
                    with pool.Fori(0, ITERS) as i:
                        n0 = pool.snap((p * ITERS + i) * SLOTS)
                        h0 = pool.snap((p * ITERS + i) * 2)
                        for s in range(SLOTS):
                            if s % HALF == 0:
                                pool.wait_ge(l["staged"], h0 + (s // HALF + 1))
                            pool.wait_ge(used.sem, used.after(n0 + (s - SLOTS)))
                            pool.sem_inc(l["issued"], 1)
                            for j in range(QT):
                                c = (s % HALF) * QT + j
                                nc.gpsimd.indirect_dma_start(
                                    rows[:, s, j, :], None, table,
                                    bass.IndirectOffsetOnAxis(ap=idx_stage[:, s // HALF, c:c + 1], axis=0),
                                ).then_inc(l["gathered"][s], 16)

            pool.wait_ge(s_tab, 1)
            pool.wait_ge(aw[0], 16 * (GROUPS // 2 + 1))
            pool.wait_ge(aw[1], 16 * (GROUPS // 2))
            gather(0, src_rows)

            def write_relations(G):
                pool.wait_ge(u_x1.sem, u_x1.after(G.g))
                pool.sem_inc(gm, 1)
                if G.tail:
                    nc.gpsimd.tensor_copy(x1[:, GROUPS * GB, :], x1s[:, 0, 0, :]).then_inc(u_x1k.sem, 1)
                else:
                    nc.gpsimd.tensor_copy(x1[:, bass.ds(G.g * GB, GB), :], x1s[:, G.b, :, :]).then_inc(u_x1k.sem, 1)
                for k in range(G.nb):
                    n = G.g * GB + k
                    pool.wait_ge(u_hc0.sem, u_hc0.after(n))
                    pool.wait_ge(u_hc1.sem, u_hc1.after(n))
                    pool.sem_inc(gm, 1)
                    pool.dma_start(rel_blocks[:, bass.ds(n, 1), :], hs[:, k % 2:k % 2 + 1, :]).then_inc(u_hw[k % 2], 16)
            groups(pool, write_relations)
            pool.wait_ge(u_hw[0], 16 * (GROUPS * 2 + 1))
            pool.wait_ge(u_hw[1], 16 * (GROUPS * 2))
            gather(1, rel_rows)

        @block.tensor
        def _(pe):
            pe.wait_ge(s_const, 10)
            pe.wait_ge(s_cast, 3)
            for k in range(4):
                for c in range(CH):
                    t = rawf[:, k, c, :] if k < 3 else raw_w[:, c, :]
                    ins = nc.tensor.transpose(bank[2 * k + c // 4][:, (c % 4) * P:(c % 4 + 1) * P], t, ident[:, :])
                ins.then_inc(s_etr, 1)
            pe.wait_ge(s_base, 1)
            pe.wait_ge(s_ecp, 8)
            nc.tensor.matmul(bank[0][:, 0:QUADS], ones[0:1, :], win_f, start=True, stop=True).then_inc(s_baseb, 1)
            pe.wait_ge(s_nfar, 1)
            nc.tensor.matmul(bank[1][0:1, 0:1], n_far[:, :], ones[:, 0:1], start=True, stop=True).then_inc(s_nfars, 1)
            start_credits(pe, xtr, abm, u_tr, u_mm, u_t1, u_root, u_h0, u_h1, u_ct, f_tr)
            pe.wait_ge(s_w, 16 * 11)
            pe.wait_ge(s_tab, 1)

            def prepare(G):
                pe.wait_ge(xl[G.b], G.pair * 16 + 16)
                pe.wait_ge(xtc.sem, xtc.after(G.g - 2))
                for k in range(G.nb):
                    ins = nc.tensor.transpose(bank[G.b][:, k * P:(k + 1) * P], xs[:, G.b, k, :], ident[:, :])
                ins.then_inc(xtr.sem, 1)
                pe.wait_ge(xtc.sem, xtc.after(G.g))
                pe.wait_ge(ac.sem, ac.after(G.g - 2))
                pe.wait_ge(bc.sem, bc.after(G.g - 2))
                for part in range(2):
                    for k in range(G.nb):
                        ins = nc.tensor.matmul(bank[2 + 2 * part + G.b][:, k * P:(k + 1) * P], xT[:, G.b, k, :],
                                               w_ab[:, part, :], start=True, stop=True)
                ins.then_inc(abm.sem, 1)
            groups(pe, prepare)

            def edge_loop(k):
                l = L[k]
                start_credits(pe, l["onehot_turned"], l["looked_up"], l["scattered"])
                passes = pe.value_load(passes_i[0:1, 0:1], min_val=1, max_val=PASSES)
                with pe.Fori(0, passes) as p:
                    at, step = pass_values(pe, p)
                    with pe.Fori(0, ITERS) as i:
                        n0 = pe.snap((p * ITERS + i) * SLOTS)

                        def turn(s):
                            b, n = s % 2, n0 + s
                            pe.wait_ge(l["onehot_ready"].sem, l["onehot_ready"].after(n))
                            pe.wait_ge(l["turned_copied"].sem, l["turned_copied"].after(n - 2))
                            for j in range(QT):
                                ins = nc.tensor.transpose(bank[b][:, j * P:(j + 1) * P], onehot[:, s % 4, j, :], ident[:, :])
                            ins.then_inc(l["onehot_turned"].sem, 1)

                        def look_up(s):
                            b, n = s % 2, n0 + s
                            w = window_of(pe, i, s, at, step)
                            pe.wait_ge(l["turned_copied"].sem, l["turned_copied"].after(n))
                            pe.wait_ge(l["lookup_used"].sem, l["lookup_used"].after(n - 2))
                            if k == 0:
                                table = tgt_win.rearrange("p q h k c -> p (q h) (k c)")
                                for j in range(QT):
                                    for h in range(3):
                                        ins = nc.tensor.matmul(
                                            bank[2 + b][:, j * P:(j + 1) * P], onehot_t[:, b, j, :],
                                            table[:, bass.ds(w, 1), h * C:(h + 1) * C],
                                            start=(h == 0), stop=(h == 2))
                            else:
                                table = inv_win[:, :, :, :, :].rearrange("p q h k r -> p (q h) (k r)")
                                for j in range(QT):
                                    ins = nc.tensor.matmul(bank[2 + b][:, j * 3 * R:(j + 1) * 3 * R], onehot_t[:, b, j, :],
                                                           table[:, bass.ds(w, 1), :], start=True, stop=True)
                            ins.then_inc(l["looked_up"].sem, 1)

                        def scatter(s):
                            b, n = s % 2, n0 + s
                            pe.wait_ge(l["messages_ready"].sem, l["messages_ready"].after(n))
                            pe.wait_ge(l["window_added"].sem, l["window_added"].after(n - 2))
                            for j in range(QT):
                                ins = nc.tensor.matmul(bank[4 + b][:, 0:P], msg[:, b, j, :], onehot[:, s % 4, j, :],
                                                       start=(j == 0), stop=(j == QT - 1))
                            if k == 0:
                                pe.wait_ge(l["counts_added"].sem, l["counts_added"].after(n - 2))
                                for j in range(QT):
                                    ins = nc.tensor.matmul(bank[6 + b][0:R, 0:P], types[:, s % 4, j, 0, :], onehot[:, s % 4, j, :],
                                                           start=(j == 0), stop=(j == QT - 1))
                            ins.then_inc(l["scattered"].sem, 1)

                        turn(0)
                        for s in range(SLOTS):
                            if s + 1 < SLOTS:
                                turn(s + 1)
                            look_up(s)
                            if s >= 1:
                                scatter(s - 1)
                        scatter(SLOTS - 1)

            pe.wait_ge(ac.sem, ac.after(GROUPS))
            pe.wait_ge(bc.sem, bc.after(GROUPS))
            pe.wait_ge(s_odd, 32)
            edge_loop(0)

            pe.wait_ge(l_done[0], 1)

            def update(G):
                pe.wait_ge(ul[G.b], G.pair * 16 + 16)
                pe.wait_ge(u_tc.sem, u_tc.after(G.g - 1))
                for k in range(G.nb):
                    ins = nc.tensor.transpose(bank[0][:, k * P:(k + 1) * P], xs[:, G.b, k, :], ident[:, :])
                ins.then_inc(u_tr.sem, 1)
                pe.wait_ge(u_cs.sem, u_cs.after(G.g))
                pe.wait_ge(u_iv.sem, u_iv.after(G.g - 1))
                pe.sem_inc(gm, 1)
                for k in range(2 * G.nb):
                    ins = nc.tensor.transpose(bank[1][:, k * R:(k + 1) * R], cs[G.b][:, k * (P // 2):k * (P // 2) + P],
                                              ident[0:R, 0:R])
                ins.then_inc(u_ct.sem, 1)
                pe.wait_ge(u_tc.sem, u_tc.after(G.g))
                pe.wait_ge(u_st.sem, u_st.after(G.g))
                pe.wait_ge(u_y.sem, u_y.after(G.g - 1))
                for k in range(G.nb):
                    nc.tensor.matmul(bank[2][:, k * P:(k + 1) * P], xT[:, G.b, k, :], w_self[:, :], start=True, stop=True)
                    nc.tensor.matmul(bank[3][:, k * P:(k + 1) * P], xT[:, G.b, k, :], w_up[:, 0, :], start=True, stop=False)
                    ins = nc.tensor.matmul(bank[3][:, k * P:(k + 1) * P], aT[:, G.b, k, :], w_up[:, 1, :], start=False, stop=True)
                ins.then_inc(u_mm.sem, 1)

            def relations(G):
                pe.wait_ge(u_x1.sem, u_x1.after(G.g))
                pe.wait_ge(u_t1c.sem, u_t1c.after(G.g - 1))
                for k in range(G.nb):
                    ins = nc.tensor.transpose(bank[4][:, k * P:(k + 1) * P], x1s[:, G.b, k, :], ident[:, :])
                ins.then_inc(u_t1.sem, 1)
                pe.wait_ge(u_t1c.sem, u_t1c.after(G.g))
                pe.wait_ge(u_rootc.sem, u_rootc.after(G.g - 1))
                nc.tensor.matmul(bank[5][:, 0:G.nb * P], w_ro[:, :], x1T[:, 0:G.nb, :], start=True, stop=True).then_inc(u_root.sem, 1)
                for k in range(G.nb):
                    n = G.g * GB + k
                    for h, (done, copied) in enumerate(((u_h0, u_hc0), (u_h1, u_hc1))):
                        pe.wait_ge(copied.sem, copied.after(n - 1))
                        nc.tensor.matmul(bank[6 + h][:, :], x1T[:, k, :], w_r[:, h * (R // 2):(h + 1) * (R // 2), :],
                                         start=True, stop=True).then_inc(done.sem, 1)
            skewed(pe, update, relations)

            pe.wait_ge(u_rootc.sem, u_rootc.after(GROUPS))
            pe.wait_ge(u_hc0.sem, u_hc0.after(GROUPS * GB))
            pe.wait_ge(u_hc1.sem, u_hc1.after(GROUPS * GB))
            pe.wait_ge(c_upd, (GROUPS + 1) * UPD_STEPS)
            edge_loop(1)

            def turn_back(G):
                pe.wait_ge(f_m.sem, f_m.after(G.g))
                pe.wait_ge(f_y.sem, f_y.after(G.g - 2))
                for k in range(G.nb):
                    ins = nc.tensor.transpose(bank[G.b][:, k * P:(k + 1) * P], cap[:, G.b, k, :], ident[:, :])
                ins.then_inc(f_tr.sem, 1)
            pe.wait_ge(l_done[1], 1)
            groups(pe, turn_back)

        @block.scalar
        def _(act):
            for k, d in enumerate((src_f, dst_f, type_f, dist)):
                act.wait_ge(s_etr, k + 1)
                nc.scalar.copy(d[:, 0:512], bank[2 * k][:, :]).then_inc(s_ecp, 1)
                nc.scalar.copy(d[:, 512:COLS], bank[2 * k + 1][:, 0:COLS - 512]).then_inc(s_ecp, 1)
            start_credits(act, xtc, ac, u_tc, u_sd, u_t1c, u_rootc, u_hc0, f_z, f_exp)

            def prepare(G):
                b, nb = G.b, G.nb
                act.wait_ge(xtr.sem, xtr.after(G.g))
                act.wait_ge(abm.sem, abm.after(G.g - 2))
                nc.scalar.copy(xT[:, b, 0:nb, :], bank[b][:, 0:nb * P].rearrange("p (k c) -> p k c", c=C)).then_inc(xtc.sem, 1)
                if not G.first:
                    act.wait_ge(aw[b], G.pair * 16)
                act.wait_ge(abm.sem, abm.after(G.g))
                nc.scalar.copy(a_out[:, b, 0:nb, :], bank[2 + b][:, 0:nb * P].rearrange("p (k c) -> p k c", c=C)).then_inc(ac.sem, 1)
            groups(act, prepare)

            def edge_loop(k):
                l = L[k]
                start_credits(act, l["turned_copied"], l["messages_ready"], *([l["used"]] if k else []))
                passes = act.value_load(passes_i[0:1, 0:1], min_val=1, max_val=PASSES)
                with act.Fori(0, passes) as p:
                    with act.Fori(0, ITERS) as i:
                        it = act.snap(p * ITERS + i)
                        n0 = act.snap(it * SLOTS)

                        def copy_turned(s):
                            b, n = s % 2, n0 + s
                            act.wait_ge(l["onehot_turned"].sem, l["onehot_turned"].after(n))
                            act.wait_ge(l["looked_up"].sem, l["looked_up"].after(n - 2))
                            nc.scalar.copy(onehot_t[:, b, :, :], bank[b][:, :].rearrange("p (k c) -> p k c", c=P)
                                           ).then_inc(l["turned_copied"].sem, 1)

                        def message(s):
                            b, n = s % 2, n0 + s
                            act.wait_ge(l["scattered"].sem, l["scattered"].after(n - 2))
                            act.wait_ge(l["lookup_used"].sem, l["lookup_used"].after(n))
                            if k == 0:
                                nc.scalar.activation(msg[:, b, :, :], pre[:, b, :, :], ACT.Relu).then_inc(l["messages_ready"].sem, 1)
                            else:
                                act.wait_ge(l["gathered"][s], (it + 1) * (16 * QT))
                                for j in range(QT):
                                    ins = nc.scalar.activation(msg[:, b, j, :], rows[:, s, j, :], ACT.Copy,
                                                               scale=edge_w[:, b, j:j + 1])
                                ins.then_inc(l["messages_ready"].sem, 1)
                                act.wait_ge(l["messages_ready"].sem, l["messages_ready"].after(n))
                                act.sem_inc(l["used"].sem, 1)

                        copy_turned(0)
                        for s in range(SLOTS):
                            if s + 1 < SLOTS:
                                copy_turned(s + 1)
                            message(s)
            edge_loop(0)

            def update(G):
                b, nb = G.b, G.nb
                act.wait_ge(u_tr.sem, u_tr.after(G.g))
                act.wait_ge(u_mm.sem, u_mm.after(G.g - 2))
                nc.scalar.copy(xT[:, b, 0:nb, :], bank[0][:, 0:nb * P].rearrange("p (k c) -> p k c", c=C)).then_inc(u_tc.sem, 1)
                act.wait_ge(u_var.sem, u_var.after(G.g))
                nc.scalar.activation(sd[:, 0:nb], vare[:, 0:nb], ACT.Sqrt).then_inc(u_sd.sem, 1)

            def relations(G):
                nb = G.nb
                act.wait_ge(u_t1.sem, u_t1.after(G.g))
                act.wait_ge(u_h1.sem, u_h1.after(G.g * GB - 1))
                nc.scalar.copy(x1T[:, 0:nb, :], bank[4][:, 0:nb * P].rearrange("p (k c) -> p k c", c=C)).then_inc(u_t1c.sem, 1)
                act.wait_ge(u_root.sem, u_root.after(G.g))
                act.sem_inc(gm, 1)
                nc.scalar.activation(agg[:, bass.ds(G.g * (GB * P), nb * P)], bank[5][:, 0:nb * P], ACT.Identity,
                                     bias=chan[:, 0:1]).then_inc(u_rootc.sem, 1)
                for k in range(nb):
                    if not (isinstance(G.g, int) and G.g == 0 and k < 2):
                        act.wait_ge(u_hw[k % 2], (G.g * 2 + k // 2) * 16)
                    act.wait_ge(u_h0.sem, u_h0.after(G.g * GB + k))
                    nc.scalar.copy(hs[:, k % 2, 0:R * C // 2], bank[6][:, :]).then_inc(u_hc0.sem, 1)
            skewed(act, update, relations)
            edge_loop(1)

            act.wait_ge(s_bv, 1)
            nc.scalar.activation(baff[:, 1:2], baff[:, 0:1], ACT.Sqrt).then_inc(s_bsd, 1)
            act.wait_ge(s_aff, 1)

            def exponential(G):
                b, nb = G.b, G.nb
                act.wait_ge(f_m.sem, f_m.after(G.g - 2))
                act.sem_inc(gm, 1)
                nc.scalar.activation(zb[:, b, 0:nb, :], agg[:, bass.ds(G.g * (GB * P), nb * P)].rearrange("p (k c) -> p k c", c=P),
                                     ACT.Identity, bias=baff[:, 4:5], scale=baff[:, 3:4]).then_inc(f_z.sem, 1)
                act.wait_ge(f_cap.sem, f_cap.after(G.g))
                nc.scalar.activation(ez[:, b, 0:nb, :], cap[:, b, 0:nb, :], ACT.Exp).then_inc(f_exp.sem, 1)
            groups(act, exponential)
            act.wait_ge(s_fv, 1)
            nc.scalar.activation(sdall[:, 1, :], sdall[:, 0, :], ACT.Sqrt).then_inc(s_fsd, 1)

        @block.vector
        def _(dve):
            v = nc.vector
            for k, pad in enumerate((0, FAR, 0)):
                v.memset(raw[:, k, CH - 1, :], pad).then_inc(s_pad, 1)
            v.memset(raw_w[:, CH - 1, :], 0.0).then_inc(s_pad, 1)
            v.memset(tgt_win[P // 2:P, BLOCKS - 1, 1, :, :], 0.0).then_inc(s_clear, 1)
            dve.wait_ge(s_edges, 16 * 12)
            for k in range(3):
                v.tensor_copy(rawf[:, k, :, :], raw[:, k, :, :]).then_inc(s_cast, 1)
            dve.wait_ge(s_ecp, 8)
            ch = Chain(dve, c_edge)
            for o, n in ((0, TILES), (TILES, BODY_T)):
                ch.step(v.tensor_copy(idx[0][:, o:o + n], src_f[:, 0:n]))
                ch.step(v.scalar_tensor_tensor(out=idx[1][:, o:o + n], in0=src_f[:, 0:n], scalar=float(R),
                                               in1=type_f[:, 0:n], op0=ALU.mult, op1=ALU.add))
            ch.step(v.tensor_copy(first_i, dst_f[0:1, 0:TILES:QT]))
            ch.step(v.tensor_scalar(win_tab[0:1, 0:QUADS], first_i, 6, None, ALU.arith_shift_right))
            v.tensor_scalar(win_f, win_tab[0:1, 0:QUADS], 64.0, None, ALU.mult).then_inc(s_base, 1)
            dve.wait_ge(s_baseb, 1)
            ch.step(v.tensor_tensor(rel0[:, :].rearrange("p (q j) -> p q j", j=QT),
                                    dst_f[:, 0:TILES].rearrange("p (q j) -> p q j", j=QT),
                                    bank[0][:, 0:QUADS].unsqueeze(2).broadcast_to([P, QUADS, QT]), ALU.subtract))
            ch.step(v.tensor_scalar(outside[:, :], rel0[:, :], 0.0, None, ALU.is_ge))
            ch.step(v.scalar_tensor_tensor(out=inside, in0=rel0[:, :], scalar=float(P), in1=outside[:, :],
                                           op0=ALU.is_lt, op1=ALU.mult))
            ch.step(v.scalar_tensor_tensor(out=outside[:, :], in0=dst_f[:, 0:TILES], scalar=float(FAR // 2), in1=inside,
                                           op0=ALU.is_lt, op1=ALU.subtract))
            v.reduce_sum(n_far[:, :], outside[:, :], AX.X).then_inc(s_nfar, 1)
            ch.step(v.scalar_tensor_tensor(out=far0[:, :], in0=dst_f[:, 0:TILES], scalar=float(FAR), in1=outside[:, :],
                                           op0=ALU.add, op1=ALU.mult))
            ch.step(v.tensor_scalar(far0[:, :], far0[:, :], float(-FAR), None, ALU.add))
            dve.wait_ge(s_nfars, 1)
            ch.step(v.tensor_scalar(passes_f[:, 0:1], bank[1][0:1, 0:1], 1.0, float(BLOCKS), ALU.min, ALU.mult))
            v.tensor_scalar(passes_i[:, :], passes_f[:, 0:1], 1.0, None, ALU.add).then_inc(s_tab, 1)
            start_credits(dve, bc, u_st, u_cs, u_y, u_var, u_x1, u_hc1, u_iv, f_cap, f_m, f_y, f_n)
            pool_credits = (u_x1k,)
            start_credits(dve, *pool_credits)
            dve.wait_ge(s_w, 16 * 11)

            def prepare(G):
                nb = G.nb
                ch = Chain(dve, c_prep, G.g * 6)
                if G.tail:
                    dve.wait_ge(xtr.sem, xtr.after(GROUPS - 2))
                    v.memset(xs[LAST // 32 * 32:, 0, 0, :], 0.0).then_inc(s_tail, 1)
                dve.wait_ge(abm.sem, abm.after(G.g))
                part = bsum[:, 0:nb, :]
                ins = v.tensor_tensor(part, bank[4 + G.b][:, 0:nb * P].rearrange("p (k c) -> p k c", c=C), over(bmsg, nb), ALU.add)
                ch.step(ins)
                dve.sem_inc(bc.sem, 1)
                ch.step(v.tensor_copy(b3[:, 0:nb, 0, :], part))
                ch.step(v.tensor_tensor(bres[:, 0:nb, :], part, b3[:, 0:nb, 0, :], ALU.subtract))
                ch.step(v.tensor_copy(b3[:, 0:nb, 1, :], bres[:, 0:nb, :]))
                ch.step(v.tensor_tensor(b3[:, 0:nb, 2, :], bres[:, 0:nb, :], b3[:, 0:nb, 1, :], ALU.subtract))
                ch.step(v.tensor_copy(tgt_win[:, bass.ds(G.g * GB, nb), 0, :, :].rearrange("p q k c -> p q (k c)"),
                                      b3[:, 0:nb, :, :].rearrange("p q k c -> p q (k c)")))
            groups(dve, prepare)

            def edge_loop(k):
                l = L[k]
                start_credits(dve, *(l[s] for s in ("onehot_ready", "lookup_used", "picked_ready", "window_added", "counts_added")),
                              *([l["used"]] if not k else []))
                v.tensor_copy(rel[:, :], rel0[:, :]).then_inc(l["targets"], 1)
                v.tensor_copy(idx_stage[:, :, :], idx[k][:, 0:BODY_T].rearrange("p (h c) -> p h c", h=2)).then_inc(l["staged"], 2)
                passes = dve.value_load(passes_i[0:1, 0:1], min_val=1, max_val=PASSES)
                with dve.Fori(0, passes) as p:
                    at, step = pass_values(dve, p)
                    dve.wait_ge(l["targets"], p + 1)
                    dve.sem_inc(gm, 1)
                    with dve.Fori(0, ITERS) as i:
                        it = dve.snap(p * ITERS + i)
                        n0 = dve.snap(it * SLOTS)

                        def one_hot(s):
                            b, n = s % 4, n0 + s
                            col = i * BODY_T + s * QT
                            dve.wait_ge(l["scattered"].sem, l["scattered"].after(n - 4))
                            for j in range(QT):
                                v.tensor_scalar(onehot[:, b, j, :], node_iota[:, :], rel[:, bass.ds(col + j, 1)], None, ALU.is_equal)
                            reps = 3 if k else 1
                            for h in range(reps):
                                ins = v.tensor_tensor(
                                    types[:, b, :, h, :], node_iota[:, 0:R].unsqueeze(1).broadcast_to([P, QT, R]),
                                    type_f[:, bass.ds(col, QT)].unsqueeze(2).broadcast_to([P, QT, R]), ALU.is_equal)
                            ins.then_inc(l["onehot_ready"].sem, 1)

                        def weigh(s):
                            b, n = s % 2, n0 + s
                            dve.wait_ge(l["messages_ready"].sem, l["messages_ready"].after(n - 2))
                            dve.wait_ge(l["gathered"][s], (it + 1) * (16 * QT))
                            for j in range(QT):
                                ins = v.scalar_tensor_tensor(
                                    out=pre[:, b, j, :], in0=w_dist[:, :], scalar=dist[:, bass.ds(i * BODY_T + (s * QT + j), 1)],
                                    in1=rows[:, s, j, :], op0=ALU.mult, op1=ALU.add)
                            ins.then_inc(l["used"].sem, 1)

                        def use_lookup(s):
                            b, n = s % 2, n0 + s
                            dve.wait_ge(l["looked_up"].sem, l["looked_up"].after(n))
                            if k == 0:
                                dve.wait_ge(l["used"].sem, l["used"].after(n))
                                v.tensor_tensor(pre[:, b, :, :], pre[:, b, :, :], bank[2 + b][:, :].rearrange("p (k c) -> p k c", c=C),
                                                ALU.add).then_inc(l["lookup_used"].sem, 1)
                            else:
                                dve.wait_ge(l["messages_ready"].sem, l["messages_ready"].after(n - 2))
                                dve.wait_ge(l["lookup_used"].sem, l["lookup_used"].after(n - 1))
                                v.tensor_tensor(picked[:, :, :], bank[2 + b][:, 0:QT * 3 * R].rearrange("p (j c) -> p j c", j=QT),
                                                types[:, s % 4, :, :, :].rearrange("p j h r -> p j (h r)"), ALU.mult
                                                ).then_inc(l["picked_ready"].sem, 1)
                                dve.wait_ge(l["picked_ready"].sem, l["picked_ready"].after(n))
                                v.reduce_sum(edge_w[:, b, :], picked[:, :, :], AX.X).then_inc(l["lookup_used"].sem, 1)

                        def add_window(s):
                            b, n = s % 2, n0 + s
                            w = window_of(dve, i, s, at, step)
                            node = dve.snap(w * (P // 2))
                            dve.wait_ge(l["scattered"].sem, l["scattered"].after(n))
                            dve.wait_ge(l["window_added"].sem, l["window_added"].after(n - 1))
                            v.tensor_tensor(agg[:, bass.ds(node, P)], agg[:, bass.ds(node, P)], bank[4 + b][:, 0:P], ALU.add
                                            ).then_inc(l["window_added"].sem, 1)
                            if k == 0:
                                dve.wait_ge(l["counts_added"].sem, l["counts_added"].after(n - 1))
                                v.tensor_tensor(cnt[:, bass.ds(node, P)], cnt[:, bass.ds(node, P)], bank[6 + b][0:R, 0:P], ALU.add
                                                ).then_inc(l["counts_added"].sem, 1)

                        def restage(h):
                            dve.wait_ge(l["messages_ready"].sem, l["messages_ready"].after(n0 + (h * HALF + HALF - 1)))
                            v.tensor_scalar(idx_stage[:, h, :], idx[k][:, bass.ds(i * BODY_T + (h * STAGE_T + BODY_T), STAGE_T)],
                                            0.0, None, ALU.add).then_inc(l["staged"], 1)

                        one_hot(0)
                        for s in range(SLOTS):
                            if s + 1 < SLOTS:
                                one_hot(s + 1)
                            if k == 0:
                                weigh(s)
                            use_lookup(s)
                            if s >= 1:
                                add_window(s - 1)
                            if s == HALF:
                                restage(0)
                        add_window(SLOTS - 1)
                        restage(1)
                    dve.wait_ge(l["onehot_ready"].sem, l["onehot_ready"].after((p + 1) * QUADS - 1))
                    v.tensor_scalar(rel[:, :], far0[:, :], moved[:, bass.ds(p, 1)], None, ALU.subtract).then_inc(l["targets"], 1)
                end = passes * QUADS - 1
                dve.wait_ge(l["window_added"].sem, l["window_added"].after(end))
                if k == 0:
                    dve.wait_ge(l["counts_added"].sem, l["counts_added"].after(end))
                dve.sem_inc(l_done[k], 1)

            dve.wait_ge(s_clear, 3)
            edge_loop(0)

            def norm_statistics(ch, values, nb):
                for k in range(nb):
                    ins = v.bn_stats(st6[:, k, :], values[:, k, :])
                ch.step(ins)
                dve.sem_inc(gm, 1)
                for k in range(nb):
                    ins = v.bn_aggr(mv[:, k, :], st6[:, k, :])
                ch.step(ins)

            def update(G):
                b, nb = G.b, G.nb
                ch = Chain(dve, c_upd, G.g * UPD_STEPS)
                if G.tail:
                    dve.wait_ge(u_y.sem, u_y.after(GROUPS - 2))
                    v.memset(xs[LAST // 32 * 32:, 0, 0, :], 0.0).then_inc(s_tail, 1)
                dve.wait_ge(u_mm.sem, u_mm.after(G.g - 2))
                v.tensor_scalar(aT[:, b, 0:nb, :], agg[:, bass.ds(G.g * (GB * P), nb * P)].rearrange("p (k c) -> p k c", c=P),
                                1.0, None, ALU.mult).then_inc(u_st.sem, 1)
                dve.wait_ge(u_ct.sem, u_ct.after(G.g - 2))
                v.tensor_scalar(cs[b][:, 0:nb * P + P // 2], cnt[:, bass.ds(G.g * (GB * P), nb * P + P // 2)],
                                1.0, None, ALU.mult).then_inc(u_cs.sem, 1)
                wn = 2 * nb
                dve.wait_ge(u_ct.sem, u_ct.after(G.g))
                ch.step(v.tensor_scalar(inv[:, 0:wn, :], bank[1][:, 0:wn * R].rearrange("p (k r) -> p k r", r=R), 1.0, None, ALU.max))
                dve.sem_inc(u_iv.sem, 1)
                ch.step(v.reciprocal(inv_r[:, 0:wn, :], inv[:, 0:wn, :]))
                ch.step(v.tensor_copy(inv3[:, 0:wn, 0, :], inv_r[:, 0:wn, :]))
                ch.step(v.tensor_tensor(inv[:, 0:wn, :], inv_r[:, 0:wn, :], inv3[:, 0:wn, 0, :], ALU.subtract))
                ch.step(v.tensor_copy(inv3[:, 0:wn, 1, :], inv[:, 0:wn, :]))
                ch.step(v.tensor_tensor(inv3[:, 0:wn, 2, :], inv[:, 0:wn, :], inv3[:, 0:wn, 1, :], ALU.subtract))
                ch.step(v.tensor_copy(inv_win[:, :, :, :, :].rearrange("p q h k r -> p (q h) (k r)")[:, bass.ds(G.g * (2 * GB), wn), :],
                                      inv3[:, 0:wn, :, :].rearrange("p w k r -> p w (k r)")))
                dve.wait_ge(u_mm.sem, u_mm.after(G.g))
                dve.wait_ge(ul[b], G.pair * 16 + 16)
                yy, y1 = y[:, 0:nb, :], y2[:, 0:nb, :]
                ch.step(v.tensor_tensor(y1, bank[3][:, 0:nb * P].rearrange("p (k c) -> p k c", c=C), over(bupd, nb), ALU.add))
                ch.step(v.scalar_tensor_tensor(out=yy, in0=y1, scalar=0.0, in1=bank[2][:, 0:nb * P].rearrange("p (k c) -> p k c", c=C),
                                               op0=ALU.max, op1=ALU.add))
                ch.step(v.tensor_tensor(yy, yy, xs[:, b, 0:nb, :], ALU.add))
                dve.sem_inc(u_y.sem, 1)
                norm_statistics(ch, y, nb)
                v.tensor_scalar(vare[:, 0:nb], mv[:, 0:nb, 1], EPS, None, ALU.add).then_inc(u_var.sem, 1)
                dve.wait_ge(u_sd.sem, u_sd.after(G.g))
                ch.step(v.reciprocal(rstd[:, 0:nb], sd[:, 0:nb]))
                dve.wait_ge(u_x1k.sem, u_x1k.after(G.g - 2))
                dve.wait_ge(u_t1.sem, u_t1.after(G.g - 2))
                for k in range(nb):
                    ins = v.tensor_scalar(x1s[:, b, k, :], y[:, k, :], mv[:, k, 0:1], rstd[:, k:k + 1], ALU.subtract, ALU.mult)
                ch.step(ins)
                dve.sem_inc(u_x1.sem, 1)

            def relations(G):
                for k in range(G.nb):
                    if not (isinstance(G.g, int) and G.g == 0 and k < 2):
                        dve.wait_ge(u_hw[k % 2], (G.g * 2 + k // 2) * 16)
                    dve.wait_ge(u_h1.sem, u_h1.after(G.g * GB + k))
                    v.tensor_copy(hs[:, k % 2, R * C // 2:], bank[7][:, :]).then_inc(u_hc1.sem, 1)
            skewed(dve, update, relations)
            dve.wait_ge(u_rootc.sem, u_rootc.after(GROUPS))
            dve.wait_ge(u_x1k.sem, u_x1k.after(GROUPS))
            edge_loop(1)

            ch = Chain(dve, c_fin)
            for c in range(NST):
                ins = v.bn_stats(bst[:, c, :], agg[:, c * SC:(c + 1) * SC])
            ch.step(ins)
            ch.step(v.bn_aggr(bmv[:, :], bst[:, :, :].rearrange("p a b -> p (a b)")))
            v.tensor_scalar(baff[:, 0:1], bmv[:, 1:2], EPS, None, ALU.add).then_inc(s_bv, 1)
            dve.wait_ge(s_bsd, 1)
            ch.step(v.reciprocal(baff[:, 2:3], baff[:, 1:2]))
            ch.step(v.tensor_tensor(baff[:, 3:4], baff[:, 2:3], chan[:, 1:2], ALU.mult))
            ch.step(v.tensor_tensor(baff[:, 5:6], bmv[:, 0:1], baff[:, 3:4], ALU.mult))
            v.tensor_tensor(baff[:, 4:5], chan[:, 2:3], baff[:, 5:6], ALU.subtract).then_inc(s_aff, 1)
            start = ch.n

            def mish(G):
                b, nb = G.b, G.nb
                ch = Chain(dve, c_fin, G.g * 8 + start)
                z, e, c = zb[:, b, 0:nb, :], ez[:, b, 0:nb, :], cap[:, b, 0:nb, :]
                dve.wait_ge(f_z.sem, f_z.after(G.g))
                dve.wait_ge(f_tr.sem, f_tr.after(G.g - 2))
                v.tensor_scalar(c, z, EXP_CAP, None, ALU.min).then_inc(f_cap.sem, 1)
                dve.wait_ge(f_exp.sem, f_exp.after(G.g))
                ch.step(v.scalar_tensor_tensor(out=e, in0=e, scalar=2.0, in1=e, op0=ALU.add, op1=ALU.mult))
                ch.step(v.tensor_scalar(c, e, 2.0, None, ALU.add))
                ch.step(v.reciprocal(c, c))
                ch.step(v.tensor_tensor(e, e, c, ALU.mult))
                ch.step(v.tensor_tensor(c, z, e, ALU.mult))
                dve.sem_inc(f_m.sem, 1)
                dve.wait_ge(f_tr.sem, f_tr.after(G.g))
                at = bass.ds(G.g * GB, nb)
                v.tensor_tensor(e, x1[:, at, :], bank[b][:, 0:nb * P].rearrange("p (k c) -> p k c", c=C), ALU.add
                                ).then_inc(f_y.sem, 1)
                dve.wait_ge(f_y.sem, f_y.after(G.g))
                v.tensor_scalar(x1[:, at, :], e, 1.0, None, ALU.mult)
                norm_statistics(ch, ez[:, b, :, :], nb)
                ch.step(v.tensor_scalar(mvall[:, at, :], mv[:, 0:nb, :], 1.0, None, ALU.mult))
            groups(dve, mish)
            v.tensor_scalar(sdall[:, 0, :], mvall[:, :, 1], EPS, None, ALU.add).then_inc(s_fv, 1)
            dve.wait_ge(s_fsd, 1)
            ch = Chain(dve, c_nrm)
            ch.step(v.reciprocal(sdall[:, 2, :], sdall[:, 1, :]))

            def normalise(G):
                if not G.first:
                    dve.wait_ge(f_o[G.b], G.pair * 16)
                for k in range(G.nb):
                    n = G.g * GB + k
                    ins = v.tensor_scalar(xs[:, G.b, k, :].unsqueeze(1), x1[:, bass.ds(n, 1), :], mvall[:, bass.ds(n, 1), 0],
                                          sdall[:, 2, bass.ds(n, 1)], ALU.subtract, ALU.mult)
                ins.then_inc(f_n.sem, 1)
            groups(dve, normalise)


_INS = ["x", "src", "dst", "edge_type_8", "edge_weight1", "L0_gnn_W_res", "L0_gnn_W_msg", "L0_gnn_b_msg", "L0_gnn_W_upd",
        "L0_gnn_b_upd", "L1_gnn_W", "L1_gnn_root", "L1_gnn_bias", "L1_gnn_gamma", "L1_gnn_beta"]


def kernel(**inputs):
    import numpy as _np
    import concourse.bacc as _bacc
    from concourse import mybir as _mybir
    from concourse.bass_utils import run_bass_kernel_spmd as _run

    nc = _bacc.Bacc("TRN2", target_bir_lowering=False, num_devices=1)
    arrays, args = {}, []
    for name in _INS:
        a = _np.ascontiguousarray(inputs[name])
        arrays[f"in_{name}_dram"] = a
        args.append(nc.dram_tensor(f"in_{name}_dram", a.shape, _mybir.dt.from_np(a.dtype), kind="ExternalInput").ap())
    args.append(nc.dram_tensor("out_0_dram", inputs["x"].shape, _mybir.dt.float32, kind="ExternalOutput").ap())
    bass_gnn(nc, *args)
    r = _run(nc, [arrays], core_ids=[0])
    return r.results[0]["out_0_dram"]
```

```python
from contextlib import ExitStack

import concourse.bass as bass
from concourse import mybir

ALU = mybir.AluOpType
ACT = mybir.ActivationFunctionType
AX = mybir.AxisListType
F32 = mybir.dt.float32
BF16 = mybir.dt.bfloat16
I32 = mybir.dt.int32

P = 128
QT = 4
SLOTS = 8
HALF = SLOTS // 2
EPS = 1e-5
FAR = 1 << 20
EXP_CAP = 20.0


class Stage:

    def __init__(self, sem, credit=2):
        self.sem, self.credit = sem, credit

    def after(self, n):
        return n + (1 + self.credit)


def bass_gnn(nc, x, src, dst, edge_type, edge_weight, w_res, w_msg, b_msg, w_upd, b_upd,
             w_rel, w_root, b_rel, gamma, beta, out):
    N, C = x.shape
    E = src.shape[0]
    R = w_rel.shape[0]
    assert C == P
    BLOCKS = -(-N // P)
    LAST = N - (BLOCKS - 1) * P
    QUADS = -(-E // (P * QT * SLOTS)) * SLOTS
    TILES = QUADS * QT
    ITERS = QUADS // SLOTS
    CH = -(-TILES // P)
    COLS = CH * P
    GB = 4
    GROUPS = BLOCKS // GB
    assert BLOCKS % GB == 1 and GROUPS % 2 == 0 and (QUADS - 1) * QT * P < E
    FULL = E // P
    NW = (BLOCKS + 1) * P
    PASSES = 1 + BLOCKS
    BODY_T = SLOTS * QT
    STAGE_T = HALF * QT
    SC = max(d for d in range(1, 513) if N % d == 0)
    NST = N // SC
    UPD_STEPS = 7

    src_rows = nc.dram_tensor("src_rows", (BLOCKS * P, C), F32).ap()
    rel_rows = nc.dram_tensor("rel_rows", (BLOCKS * P * R, C), F32).ap()

    ctx = ExitStack()
    with ctx:
        def sb(name, shape, dt=F32):
            return ctx.enter_context(nc.sbuf_tensor(name, shape, dt))

        def sem(name):
            return ctx.enter_context(nc.semaphore(name))

        bank = [ctx.enter_context(nc.psum_tensor(f"bank{i}", [P, 512], F32)) for i in range(8)]

        ident = sb("ident", [P, P])
        node_iota = sb("node_iota", [P, P])
        ones = sb("ones", [P, P])
        w_ab = sb("w_ab", [P, 2, C])
        w_dist = sb("w_dist", [P, C])
        w_self = sb("w_self", [P, C])
        w_up = sb("w_up", [P, 2, C])
        w_r = sb("w_r", [P, R, C])
        w_ro = sb("w_ro", [P, C])
        bmsg = sb("bmsg", [P, C])
        bupd = sb("bupd", [P, C])
        chan = sb("chan", [P, 3])
        onehot = sb("onehot", [P, 4, QT, P])
        onehot_mem = onehot[:, :, :, :].rearrange("p b j c -> p (b j c)")
        src_f = onehot_mem[:, 0:COLS]
        dst_f = onehot_mem[:, COLS:2 * COLS]
        type_f = sb("type_f", [P, COLS])
        dist = sb("dist", [P, COLS])
        idx = [sb(f"idx{k}", [P, TILES + BODY_T], I32) for k in range(2)]
        idx_stage = sb("idx_stage", [P, 2, STAGE_T], I32)
        rel0 = sb("rel0", [P, TILES])
        far0 = sb("far0", [P, TILES])
        rel = sb("rel", [P, TILES])
        inside = src_f[:, 0:TILES]
        moved = sb("moved", [P, PASSES])
        outside = rel
        n_far = sb("n_far", [P, 1])
        passes_f = sb("passes_f", [1, 2])
        passes_i = sb("passes_i", [1, 1], I32)
        win_tab = sb("win_tab", [1, 2 * QUADS + BLOCKS], I32)
        pass_tab = sb("pass_tab", [1, 2, PASSES], I32)
        win_mem = sb("win_mem", [P, BLOCKS * 3 * C])
        tgt_win = win_mem[:, :].bitcast(BF16).rearrange("p (q h k c) -> p q h k c", h=2, k=3, c=C)
        x1 = win_mem[:, 0:BLOCKS * C].rearrange("p (q c) -> p q c", c=C)
        inv_win = sb("inv_win", [P, BLOCKS, 2, 3, R], BF16)
        agg = sb("agg", [P, NW])
        raw = agg[:, 0:3 * COLS].bitcast(I32).rearrange("p (k c e) -> p k c e", k=3, e=P)
        raw_w = agg[:, 3 * COLS:4 * COLS].rearrange("p (c e) -> p c e", e=P)
        rawf = agg[:, 4 * COLS:7 * COLS].rearrange("p (k c e) -> p k c e", k=3, e=P)
        cnt = sb("cnt", [P, 2 * BLOCKS, R])
        rows = sb("rows", [P, SLOTS, QT, C])
        onehot_t = sb("onehot_t", [P, 2, QT, P], BF16)
        types = sb("types", [P, 4, QT, R])
        pre = sb("pre", [P, 2, QT, C])
        msg = sb("msg", [P, 2, QT, C])
        picked = sb("picked", [P, QT, 3, R])
        edge_w = sb("edge_w", [P, 2, QT])
        first_i = rows[0:1, 6, :, :].rearrange("p a b -> p (a b)")[:, 0:QUADS].bitcast(I32)
        win_f = rows[0:1, 7, :, :].rearrange("p a b -> p (a b)")[:, 0:QUADS]
        xs = rows[:, 0:2, :, :]
        xT = rows[:, 2:4, :, :]
        a_out = rows[:, 4:6, :, :]
        hs = sb("hs", [P, GB, R * C])
        bsum = msg[:, 0, :, :]
        bres = msg[:, 1, :, :]
        part_mem = sb("part_mem", [P, GB * 3 * C // 2])
        b3 = part_mem[:, :].bitcast(BF16).rearrange("p (k h c) -> p k h c", k=GB, h=3)
        x1s = onehot[:, 0:2, :, :]
        aT = pre
        x1T = part_mem[:, 0:GB * P].rearrange("p (k c) -> p k c", k=GB)
        y2 = msg[:, 0, :, :]
        y = msg[:, 1, :, :]
        st6 = sb("st6", [P, GB, 6])
        mv = sb("mv", [P, GB, 2])
        vare = sb("vare", [P, GB])
        sd = sb("sd", [P, GB])
        rstd = sb("rstd", [P, GB])
        cnt_odd = sb("cnt_odd", [P, BLOCKS, R])
        inv = sb("inv", [P, BLOCKS, R])
        inv3 = inv_win[:, :, 0, :, :]
        zb, ez, cap = pre, onehot[:, 0:2, :, :], msg
        bst = sb("bst", [P, NST, 6])
        bmv = sb("bmv", [P, 2])
        baff = sb("baff", [P, 6])
        mvall = sb("mvall", [P, BLOCKS, 2])
        sdall = far0[:, 0:3 * BLOCKS].rearrange("p (k q) -> p k q", k=3)

        s_w, s_const, s_pad, s_edges = sem("weights_loaded"), sem("constants_set"), sem("edge_padding_set"), sem("edges_loaded")
        s_cast, s_etr, s_ecp = sem("edges_cast"), sem("edges_transposed"), sem("edges_copied")
        s_base, s_baseb = sem("window_starts_ready"), sem("window_starts_spread")
        s_nfar, s_nfars, s_tab = sem("far_edges_counted"), sem("far_edges_summed"), sem("tables_ready")
        s_clear = sem("sums_cleared")
        s_tail = sem("tail_rows_zeroed")
        gm = sem("waits_taken")
        c_edge, c_prep, c_upd, c_fin, c_nrm, c_act = (sem(f"chain_{n}") for n in ("edges", "prepare", "update", "final", "norm", "act"))
        xl = [sem(f"x_loaded{i}") for i in range(2)]
        aw = [sem(f"source_part_written{i}") for i in range(2)]
        xtr, xtc, abm, ac, bc = (Stage(sem(n)) for n in (
            "x_transposed", "x_transpose_copied", "parts_multiplied", "source_part_copied", "target_part_read"))
        s_odd = sem("odd_windows_ready")
        s_oddc, c_inv, s_inv, s_oddi = sem("odd_counts_moved"), sem("chain_inverse"), sem("inverse_ready"), sem("odd_inverse_ready")
        L = [dict(
            staged=sem(f"indices_staged{k}"),
            gathered=[sem(f"gathered{k}_{s}") for s in range(SLOTS)],
            issued=sem(f"quads_issued{k}"),
            targets=sem(f"targets_ready{k}"),
            used=Stage(sem(f"rows_used{k}"), SLOTS),
            **{n: Stage(sem(f"{n}{k}")) for n in (
                "onehot_ready", "onehot_turned", "turned_copied", "looked_up", "lookup_used",
                "picked_ready", "messages_ready", "window_added", "counts_added")},
            scattered=Stage(sem(f"scattered{k}"), 4),
        ) for k in range(2)]
        l_done = [sem(f"layer_summed{k}") for k in range(2)]
        ul = [sem(f"update_x_loaded{i}") for i in range(2)]
        u_hw = [sem(f"relation_rows_written{k}") for k in range(GB)]
        (u_st, u_tr, u_tc, u_mm, u_y, u_var, u_sd, u_x1, u_x1k, u_t1, u_t1c, u_root, u_rootc, u_h0, u_h1, u_hc0, u_hc1) = (Stage(sem(n)) for n in (
            "sums_staged", "update_x_transposed", "update_x_copied", "update_multiplied", "update_y_ready",
            "update_variance_ready", "update_deviation_ready", "x1_ready", "x1_kept", "x1_transposed", "x1_transpose_copied",
            "root_multiplied", "root_added", "relations_low_multiplied", "relations_high_multiplied",
            "relations_low_copied", "relations_high_copied"))
        s_bv, s_bsd, s_aff = sem("batch_variance_ready"), sem("batch_deviation_ready"), sem("batch_affine_ready")
        f_z, f_cap, f_exp, f_u, f_d, f_r, f_t, f_m, f_tr, f_y = (Stage(sem(n)) for n in (
            "final_z_ready", "final_capped", "final_exp_ready", "final_u_ready", "final_divisor_ready", "final_reciprocal_ready", "final_ratio_ready", "final_mish_ready", "final_transposed", "final_y_read"))
        s_fv, s_fsd = sem("final_variances_ready"), sem("final_deviations_ready")
        s_scale = sem("final_scales_ready")
        f_n, f_n1 = Stage(sem("final_normalised_even")), Stage(sem("final_normalised_odd"))
        f_o = [sem(f"final_written{i}") for i in range(2)]

        x_groups = x[0:GROUPS * GB * P, :].rearrange("(q p) c -> p q c", p=P)
        src_groups = src_rows[0:GROUPS * GB * P, :].rearrange("(q p) c -> p q c", p=P)
        out_groups = out[0:GROUPS * GB * P, :].rearrange("(q p) c -> p q c", p=P)
        rel_blocks = rel_rows.rearrange("(q p r) c -> p q (r c)", p=P, r=R)

        class Group:

            def __init__(self, pair, b):
                self.pair, self.b, self.g = pair + b // 2, b % 2, pair * 2 + b
                self.first = isinstance(self.g, int) and self.g < 2
                self.tail = isinstance(self.g, int) and self.g == GROUPS
                self.nb = 1 if self.tail else GB

        def groups(eng, step):
            step(Group(0, 0))
            step(Group(0, 1))
            with eng.Fori(1, GROUPS // 2) as i:
                step(Group(i, 0))
                step(Group(i, 1))
            step(Group(GROUPS // 2, 0))

        def skewed(eng, a, b, lead=1):
            for k in range(lead):
                a(Group(0, k))
            for k in range(2):
                a(Group(0, k + lead))
                b(Group(0, k))
            with eng.Fori(1, GROUPS // 2 - 1) as i:
                for k in range(2):
                    a(Group(i, k + lead))
                    b(Group(i, k))
            for k in range(3):
                if k + lead <= 2:
                    a(Group(GROUPS // 2 - 1, k + lead))
                b(Group(GROUPS // 2 - 1, k))

        class Chain:

            def __init__(self, eng, s, base=0):
                self.eng, self.s, self.base, self.n = eng, s, base, 0

            def step(self, ins):
                self.n += 1
                ins.then_inc(self.s, 1)
                self.eng.wait_ge(self.s, self.base + self.n)

        def over(v, nb):
            return v[:, :].unsqueeze(1).broadcast_to([P, nb, C])

        def start_credits(eng, *stages):
            for s in stages:
                eng.sem_inc(s.sem, s.credit)

        def pass_values(eng, p):
            at = eng.value_load(pass_tab[0:1, 0, bass.ds(p, 1)], min_val=0, max_val=QUADS + BLOCKS - 1)
            step = eng.value_load(pass_tab[0:1, 1, bass.ds(p, 1)], min_val=0, max_val=1)
            return at, step

        def window_of(eng, i, s, at, step):
            return eng.value_load(win_tab[0:1, bass.ds(at + (i * SLOTS + s) * step, 1)], min_val=0, max_val=2 * BLOCKS - 1)

        block = ctx.enter_context(nc.Block())

        @block.sync
        def _(sp):
            first = (FULL // P) * P * P
            full = (FULL % P) * P
            sp.wait_ge(s_pad, 4)
            for k, e in enumerate((src, dst, edge_type, edge_weight)):
                d = raw[:, k, :, :] if k < 3 else raw_w
                e = e if k < 3 else e.rearrange("e a -> (e a)")
                sp.dma_start(d[:, 0:FULL // P, :], e[0:first].rearrange("(c p e) -> p c e", p=P, e=P)).then_inc(s_edges, 16)
                sp.dma_start(d[0:FULL % P, FULL // P, :],
                             e[first:first + full].rearrange("(p e) -> p e", e=P)).then_inc(s_edges, 16)
                sp.dma_start(d[FULL % P:FULL % P + 1, FULL // P, 0:E - FULL * P],
                             e[FULL * P:E].rearrange("(p e) -> p e", p=1)).then_inc(s_edges, 16)
            sp.dma_start(w_ab[:, :, :], w_msg[0:2 * C, :].rearrange("(k p) c -> p k c", p=P)).then_inc(s_w, 16)
            sp.dma_start(bmsg[:, :], b_msg.partition_broadcast(P)).then_inc(s_w, 16)
            sp.dma_start(w_dist[:, :], w_msg[2 * C, :].partition_broadcast(P)).then_inc(s_w, 16)
            sp.dma_start(w_self[:, :], w_res).then_inc(s_w, 16)
            sp.dma_start(w_up[:, :, :], w_upd.rearrange("(k p) c -> p k c", p=P)).then_inc(s_w, 16)
            sp.dma_start(bupd[:, :], b_upd.partition_broadcast(P)).then_inc(s_w, 16)
            sp.dma_start(w_r[:, :, :], w_rel.rearrange("r p c -> p r c")).then_inc(s_w, 16)
            sp.dma_start(w_ro[:, :], w_root).then_inc(s_w, 16)
            for k, v in enumerate((b_rel, gamma, beta)):
                sp.dma_start(chan[:, k:k + 1], v.rearrange("(p a) -> p a", a=1)).then_inc(s_w, 16)

            def load_x(G, loaded, used, tails):
                if G.tail:
                    sp.wait_ge(s_tail, tails)
                    sp.dma_start(xs[0:LAST, 0, 0, :], x[GROUPS * GB * P:N, :]).then_inc(loaded[0], 16)
                else:
                    sp.wait_ge(used.sem, used.after(G.g - 2))
                    sp.dma_start(xs[:, G.b, :, :], x_groups[:, bass.ds(G.g * GB, GB), :]).then_inc(loaded[G.b], 16)

            groups(sp, lambda G: load_x(G, xl, xtr, 1))
            sp.wait_ge(s_clear, 5)
            sp.wait_ge(c_prep, (GROUPS + 1) * 6)
            sp.dma_start(tgt_win[0:P // 2, :, 1, :, :], tgt_win[P // 2:P, :, 0, :, :]).then_inc(s_odd, 16)
            sp.dma_start(tgt_win[P // 2:P, 0:BLOCKS - 1, 1, :, :], tgt_win[0:P // 2, 1:BLOCKS, 0, :, :]).then_inc(s_odd, 16)

            sp.wait_ge(l_done[0], 1)
            by_block = cnt[:, :, :].rearrange("p (q h) r -> p q h r", h=2)
            sp.dma_start(cnt_odd[0:P // 2, 1:BLOCKS, :], by_block[P // 2:P, 0:BLOCKS - 1, 1, :]).then_inc(s_oddc, 16)
            sp.dma_start(cnt_odd[P // 2:P, :, :], by_block[0:P // 2, :, 1, :]).then_inc(s_oddc, 16)

            def load_update(G):
                load_x(G, ul, u_y, 2)

            def write_relations(G):
                for k in range(G.nb):
                    n = G.g * GB + k
                    sp.wait_ge(u_hc0.sem, u_hc0.after(n))
                    sp.wait_ge(u_hc1.sem, u_hc1.after(n))
                    sp.dma_start(rel_blocks[:, bass.ds(n, 1), :], hs[:, k:k + 1, :]).then_inc(u_hw[k], 16)
                if G.first and G.b == 0:
                    sp.wait_ge(s_inv, 1)
                    sp.dma_start(inv_win[0:P // 2, :, 1, :, :], inv_win[P // 2:P, :, 0, :, :]).then_inc(s_oddi, 16)
                    sp.dma_start(inv_win[P // 2:P, 0:BLOCKS - 1, 1, :, :], inv_win[0:P // 2, 1:BLOCKS, 0, :, :]).then_inc(s_oddi, 16)
            skewed(sp, load_update, write_relations, 2)

            def store(G):
                sp.wait_ge(f_n.sem, f_n.after(G.g))
                if not G.tail:
                    sp.wait_ge(f_n1.sem, f_n1.after(G.g))
                if G.tail:
                    sp.dma_start(out[GROUPS * GB * P:N, :], xs[0:LAST, 0, 0, :]).then_inc(f_o[0], 16)
                else:
                    sp.dma_start(out_groups[:, bass.ds(G.g * GB, GB), :], xs[:, G.b, :, :]).then_inc(f_o[G.b], 16)
            groups(sp, store)
            sp.wait_ge(f_o[0], 16 * (GROUPS // 2 + 1))
            sp.wait_ge(f_o[1], 16 * (GROUPS // 2))

        @block.gpsimd
        def _(pool):
            nc.gpsimd.memset(ident[:, :], 0.0).then_inc(s_const, 1)
            pool.wait_ge(s_const, 1)
            nc.gpsimd.affine_select(out=ident[:, :], in_=ident[:, :], compare_op=ALU.not_equal, fill=1.0,
                                    base=0, pattern=[[-1, P]], channel_multiplier=1).then_inc(s_const, 1)
            nc.gpsimd.iota(node_iota[:, :], [[1, P]], base=0, channel_multiplier=0,
                           allow_small_or_imprecise_dtypes=True).then_inc(s_const, 1)
            nc.gpsimd.memset(ones[:, :], 1.0).then_inc(s_const, 1)
            nc.gpsimd.iota(pass_tab[0:1, 0, 1:PASSES], [[1, BLOCKS]], base=QUADS, channel_multiplier=0).then_inc(s_const, 1)
            nc.gpsimd.memset(pass_tab[0:1, 0, 0:1], 0).then_inc(s_const, 1)
            nc.gpsimd.memset(pass_tab[0:1, 1, 1:PASSES], 0).then_inc(s_const, 1)
            nc.gpsimd.memset(pass_tab[0:1, 1, 0:1], 1).then_inc(s_const, 1)
            nc.gpsimd.iota(moved[:, :], [[P, PASSES]], base=0, channel_multiplier=0,
                           allow_small_or_imprecise_dtypes=True).then_inc(s_const, 1)
            nc.gpsimd.iota(win_tab[0:1, QUADS:QUADS + BLOCKS], [[2, BLOCKS]], base=0, channel_multiplier=0).then_inc(s_const, 1)
            nc.gpsimd.memset(cnt[:, :], 0.0).then_inc(s_clear, 1)
            pool.wait_ge(s_etr, 4)
            nc.gpsimd.memset(agg[:, :], 0.0).then_inc(s_clear, 1)

            def write_source_part(G):
                pool.wait_ge(ac.sem, ac.after(G.g))
                pool.sem_inc(gm, 1)
                if G.tail:
                    pool.dma_start(src_rows[GROUPS * GB * P:, :], a_out[:, 0, 0, :]).then_inc(aw[0], 16)
                else:
                    pool.dma_start(src_groups[:, bass.ds(G.g * GB, GB), :], a_out[:, G.b, :, :]).then_inc(aw[G.b], 16)
            groups(pool, write_source_part)

            def gather(k, table):
                l = L[k]
                used = l["used"]
                passes = pool.value_load(passes_i[0:1, 0:1], min_val=1, max_val=PASSES)
                with pool.Fori(0, passes) as p:
                    with pool.Fori(0, ITERS) as i:
                        n0 = pool.snap((p * ITERS + i) * SLOTS)
                        h0 = pool.snap((p * ITERS + i) * 2)
                        for s in range(SLOTS):
                            if s % HALF == 0:
                                pool.wait_ge(l["staged"], h0 + (s // HALF + 1))
                            pool.wait_ge(used.sem, used.after(n0 + (s - SLOTS)))
                            pool.sem_inc(l["issued"], 1)
                            for j in range(QT):
                                c = (s % HALF) * QT + j
                                nc.gpsimd.indirect_dma_start(
                                    rows[:, s, j, :], None, table,
                                    bass.IndirectOffsetOnAxis(ap=idx_stage[:, s // HALF, c:c + 1], axis=0),
                                ).then_inc(l["gathered"][s], 16)

            pool.wait_ge(s_tab, 1)
            pool.wait_ge(aw[0], 16 * (GROUPS // 2 + 1))
            pool.wait_ge(aw[1], 16 * (GROUPS // 2))
            gather(0, src_rows)

            def keep_x1(G):
                pool.wait_ge(u_x1.sem, u_x1.after(G.g))
                pool.sem_inc(gm, 1)
                if G.tail:
                    nc.gpsimd.tensor_copy(x1[:, GROUPS * GB, :], x1s[:, 0, 0, :]).then_inc(u_x1k.sem, 1)
                else:
                    nc.gpsimd.tensor_copy(x1[:, bass.ds(G.g * GB, GB), :], x1s[:, G.b, :, :]).then_inc(u_x1k.sem, 1)
            groups(pool, keep_x1)
            for k in range(GB):
                pool.wait_ge(u_hw[k], 16 * (GROUPS + (k == 0)))
            gather(1, rel_rows)

            def products(G):
                b, nb = G.b, G.nb
                pool.wait_ge(f_r.sem, f_r.after(G.g))
                nc.gpsimd.tensor_tensor(ez[:, b, 0:nb, :], ez[:, b, 0:nb, :], cap[:, b, 0:nb, :], ALU.mult).then_inc(f_t.sem, 1)
                pool.wait_ge(f_t.sem, f_t.after(G.g))
                pool.wait_ge(f_tr.sem, f_tr.after(G.g - 2))
                nc.gpsimd.tensor_tensor(cap[:, b, 0:nb, :], zb[:, b, 0:nb, :], ez[:, b, 0:nb, :], ALU.mult).then_inc(f_m.sem, 1)
            start_credits(pool, f_t, f_m)
            groups(pool, products)

        @block.tensor
        def _(pe):
            pe.wait_ge(s_const, 10)
            pe.wait_ge(s_cast, 3)
            for k in range(4):
                for c in range(CH):
                    t = rawf[:, k, c, :] if k < 3 else raw_w[:, c, :]
                    ins = nc.tensor.transpose(bank[2 * k + c // 4][:, (c % 4) * P:(c % 4 + 1) * P], t, ident[:, :])
                ins.then_inc(s_etr, 1)
            pe.wait_ge(s_base, 1)
            pe.wait_ge(s_ecp, 8)
            nc.tensor.matmul(bank[0][:, 0:QUADS], ones[0:1, :], win_f, start=True, stop=True).then_inc(s_baseb, 1)
            pe.wait_ge(s_nfar, 1)
            nc.tensor.matmul(bank[1][0:1, 0:1], n_far[:, :], ones[:, 0:1], start=True, stop=True).then_inc(s_nfars, 1)
            start_credits(pe, xtr, abm, u_tr, u_mm, u_t1, u_root, u_h0, u_h1, f_tr)
            pe.wait_ge(s_w, 16 * 11)
            pe.wait_ge(s_tab, 1)

            def prepare(G):
                pe.wait_ge(xl[G.b], G.pair * 16 + 16)
                pe.wait_ge(xtc.sem, xtc.after(G.g - 2))
                for k in range(G.nb):
                    ins = nc.tensor.transpose(bank[G.b][:, k * P:(k + 1) * P], xs[:, G.b, k, :], ident[:, :])
                ins.then_inc(xtr.sem, 1)
                pe.wait_ge(xtc.sem, xtc.after(G.g))
                pe.wait_ge(ac.sem, ac.after(G.g - 2))
                pe.wait_ge(bc.sem, bc.after(G.g - 2))
                for part in range(2):
                    for k in range(G.nb):
                        ins = nc.tensor.matmul(bank[2 + 2 * part + G.b][:, k * P:(k + 1) * P], xT[:, G.b, k, :],
                                               w_ab[:, part, :], start=True, stop=True)
                ins.then_inc(abm.sem, 1)
            groups(pe, prepare)

            def edge_loop(k):
                l = L[k]
                start_credits(pe, l["onehot_turned"], l["looked_up"], l["scattered"])
                passes = pe.value_load(passes_i[0:1, 0:1], min_val=1, max_val=PASSES)
                with pe.Fori(0, passes) as p:
                    at, step = pass_values(pe, p)
                    with pe.Fori(0, ITERS) as i:
                        n0 = pe.snap((p * ITERS + i) * SLOTS)

                        def turn(s):
                            b, n = s % 2, n0 + s
                            pe.wait_ge(l["onehot_ready"].sem, l["onehot_ready"].after(n))
                            pe.wait_ge(l["turned_copied"].sem, l["turned_copied"].after(n - 2))
                            for j in range(QT):
                                ins = nc.tensor.transpose(bank[b][:, j * P:(j + 1) * P], onehot[:, s % 4, j, :], ident[:, :])
                            ins.then_inc(l["onehot_turned"].sem, 1)

                        def look_up(s):
                            b, n = s % 2, n0 + s
                            w = window_of(pe, i, s, at, step)
                            pe.wait_ge(l["turned_copied"].sem, l["turned_copied"].after(n))
                            pe.wait_ge(l["lookup_used"].sem, l["lookup_used"].after(n - 2))
                            if k == 0:
                                table = tgt_win.rearrange("p q h k c -> p (q h) (k c)")
                                for j in range(QT):
                                    for h in range(3):
                                        ins = nc.tensor.matmul(
                                            bank[2 + b][:, j * P:(j + 1) * P], onehot_t[:, b, j, :],
                                            table[:, bass.ds(w, 1), h * C:(h + 1) * C],
                                            start=(h == 0), stop=(h == 2))
                            else:
                                table = inv_win[:, :, :, :, :].rearrange("p q h k r -> p (q h) (k r)")
                                for j in range(QT):
                                    ins = nc.tensor.matmul(bank[2 + b][:, j * 3 * R:(j + 1) * 3 * R], onehot_t[:, b, j, :],
                                                           table[:, bass.ds(w, 1), :], start=True, stop=True)
                            ins.then_inc(l["looked_up"].sem, 1)

                        def scatter(s):
                            b, n = s % 2, n0 + s
                            pe.wait_ge(l["messages_ready"].sem, l["messages_ready"].after(n))
                            pe.wait_ge(l["window_added"].sem, l["window_added"].after(n - 2))
                            for j in range(QT):
                                ins = nc.tensor.matmul(bank[4 + b][:, 0:P], msg[:, b, j, :], onehot[:, s % 4, j, :],
                                                       start=(j == 0), stop=(j == QT - 1))
                            if k == 0:
                                pe.wait_ge(l["counts_added"].sem, l["counts_added"].after(n - 2))
                                for j in range(QT):
                                    ins = nc.tensor.matmul(bank[6 + b][:, 0:R], onehot[:, s % 4, j, :], types[:, s % 4, j, :],
                                                           start=(j == 0), stop=(j == QT - 1))
                            ins.then_inc(l["scattered"].sem, 1)

                        turn(0)
                        for s in range(SLOTS):
                            if s + 1 < SLOTS:
                                turn(s + 1)
                            look_up(s)
                            if s >= 1:
                                scatter(s - 1)
                        scatter(SLOTS - 1)

            pe.wait_ge(ac.sem, ac.after(GROUPS))
            pe.wait_ge(bc.sem, bc.after(GROUPS))
            pe.wait_ge(s_odd, 32)
            edge_loop(0)

            pe.wait_ge(l_done[0], 1)

            def update(G):
                pe.wait_ge(ul[G.b], G.pair * 16 + 16)
                pe.wait_ge(u_tc.sem, u_tc.after(G.g - 1))
                for k in range(G.nb):
                    ins = nc.tensor.transpose(bank[0][:, k * P:(k + 1) * P], xs[:, G.b, k, :], ident[:, :])
                ins.then_inc(u_tr.sem, 1)
                pe.wait_ge(u_tc.sem, u_tc.after(G.g))
                pe.wait_ge(u_st.sem, u_st.after(G.g))
                pe.wait_ge(u_y.sem, u_y.after(G.g - 1))
                for k in range(G.nb):
                    nc.tensor.matmul(bank[2][:, k * P:(k + 1) * P], xT[:, G.b, k, :], w_self[:, :], start=True, stop=True)
                    nc.tensor.matmul(bank[3][:, k * P:(k + 1) * P], xT[:, G.b, k, :], w_up[:, 0, :], start=True, stop=False)
                    ins = nc.tensor.matmul(bank[3][:, k * P:(k + 1) * P], aT[:, G.b, k, :], w_up[:, 1, :], start=False, stop=True)
                ins.then_inc(u_mm.sem, 1)

            def relations(G):
                pe.wait_ge(u_x1.sem, u_x1.after(G.g))
                pe.wait_ge(u_t1c.sem, u_t1c.after(G.g - 1))
                for k in range(G.nb):
                    ins = nc.tensor.transpose(bank[4][:, k * P:(k + 1) * P], x1s[:, G.b, k, :], ident[:, :])
                ins.then_inc(u_t1.sem, 1)
                pe.wait_ge(u_t1c.sem, u_t1c.after(G.g))
                pe.wait_ge(u_rootc.sem, u_rootc.after(G.g - 1))
                nc.tensor.matmul(bank[5][:, 0:G.nb * P], w_ro[:, :], x1T[:, 0:G.nb, :], start=True, stop=True).then_inc(u_root.sem, 1)
                for k in range(G.nb):
                    n = G.g * GB + k
                    for h, (done, copied) in enumerate(((u_h0, u_hc0), (u_h1, u_hc1))):
                        pe.wait_ge(copied.sem, copied.after(n - 1))
                        nc.tensor.matmul(bank[6 + h][:, :], x1T[:, k, :], w_r[:, h * (R // 2):(h + 1) * (R // 2), :],
                                         start=True, stop=True).then_inc(done.sem, 1)
            skewed(pe, update, relations)

            pe.wait_ge(u_rootc.sem, u_rootc.after(GROUPS))
            pe.wait_ge(u_hc0.sem, u_hc0.after(GROUPS * GB))
            pe.wait_ge(u_hc1.sem, u_hc1.after(GROUPS * GB))
            pe.wait_ge(c_upd, (GROUPS + 1) * UPD_STEPS)
            pe.wait_ge(s_oddi, 32)
            edge_loop(1)

            def turn_back(G):
                pe.wait_ge(f_m.sem, f_m.after(G.g))
                pe.wait_ge(f_y.sem, f_y.after(G.g - 2))
                for k in range(G.nb):
                    ins = nc.tensor.transpose(bank[G.b][:, k * P:(k + 1) * P], cap[:, G.b, k, :], ident[:, :])
                ins.then_inc(f_tr.sem, 1)
            pe.wait_ge(l_done[1], 1)
            groups(pe, turn_back)

        @block.scalar
        def _(act):
            for k, d in enumerate((src_f, dst_f, type_f, dist)):
                act.wait_ge(s_etr, k + 1)
                nc.scalar.copy(d[:, 0:512], bank[2 * k][:, :]).then_inc(s_ecp, 1)
                nc.scalar.copy(d[:, 512:COLS], bank[2 * k + 1][:, 0:COLS - 512]).then_inc(s_ecp, 1)
            start_credits(act, xtc, ac, u_tc, u_sd, u_t1c, u_rootc, u_hc0, u_hc1, f_z, f_exp, f_d, f_n1)

            def prepare(G):
                b, nb = G.b, G.nb
                act.wait_ge(xtr.sem, xtr.after(G.g))
                act.wait_ge(abm.sem, abm.after(G.g - 2))
                nc.scalar.copy(xT[:, b, 0:nb, :], bank[b][:, 0:nb * P].rearrange("p (k c) -> p k c", c=C)).then_inc(xtc.sem, 1)
                if not G.first:
                    act.wait_ge(aw[b], G.pair * 16)
                act.wait_ge(abm.sem, abm.after(G.g))
                nc.scalar.copy(a_out[:, b, 0:nb, :], bank[2 + b][:, 0:nb * P].rearrange("p (k c) -> p k c", c=C)).then_inc(ac.sem, 1)
            groups(act, prepare)

            def edge_loop(k):
                l = L[k]
                start_credits(act, l["turned_copied"], l["messages_ready"], *([l["used"]] if k else []))
                passes = act.value_load(passes_i[0:1, 0:1], min_val=1, max_val=PASSES)
                with act.Fori(0, passes) as p:
                    with act.Fori(0, ITERS) as i:
                        it = act.snap(p * ITERS + i)
                        n0 = act.snap(it * SLOTS)

                        def copy_turned(s):
                            b, n = s % 2, n0 + s
                            act.wait_ge(l["onehot_turned"].sem, l["onehot_turned"].after(n))
                            act.wait_ge(l["looked_up"].sem, l["looked_up"].after(n - 2))
                            nc.scalar.copy(onehot_t[:, b, :, :], bank[b][:, :].rearrange("p (k c) -> p k c", c=P)
                                           ).then_inc(l["turned_copied"].sem, 1)

                        def message(s):
                            b, n = s % 2, n0 + s
                            act.wait_ge(l["scattered"].sem, l["scattered"].after(n - 2))
                            act.wait_ge(l["lookup_used"].sem, l["lookup_used"].after(n))
                            if k == 0:
                                nc.scalar.activation(msg[:, b, :, :], pre[:, b, :, :], ACT.Relu).then_inc(l["messages_ready"].sem, 1)
                            else:
                                act.wait_ge(l["gathered"][s], (it + 1) * (16 * QT))
                                for j in range(QT):
                                    ins = nc.scalar.activation(msg[:, b, j, :], rows[:, s, j, :], ACT.Copy,
                                                               scale=edge_w[:, b, j:j + 1])
                                ins.then_inc(l["messages_ready"].sem, 1)
                                act.wait_ge(l["messages_ready"].sem, l["messages_ready"].after(n))
                                act.sem_inc(l["used"].sem, 1)

                        copy_turned(0)
                        for s in range(SLOTS):
                            if s + 1 < SLOTS:
                                copy_turned(s + 1)
                            message(s)
            edge_loop(0)

            def update(G):
                b, nb = G.b, G.nb
                act.wait_ge(u_tr.sem, u_tr.after(G.g))
                act.wait_ge(u_mm.sem, u_mm.after(G.g - 2))
                nc.scalar.copy(xT[:, b, 0:nb, :], bank[0][:, 0:nb * P].rearrange("p (k c) -> p k c", c=C)).then_inc(u_tc.sem, 1)

            def relations(G):
                nb = G.nb
                act.wait_ge(u_t1.sem, u_t1.after(G.g))
                act.wait_ge(u_h1.sem, u_h1.after(G.g * GB - 1))
                nc.scalar.copy(x1T[:, 0:nb, :], bank[4][:, 0:nb * P].rearrange("p (k c) -> p k c", c=C)).then_inc(u_t1c.sem, 1)
                act.wait_ge(u_root.sem, u_root.after(G.g))
                act.sem_inc(gm, 1)
                nc.scalar.activation(agg[:, bass.ds(G.g * (GB * P), nb * P)], bank[5][:, 0:nb * P], ACT.Identity,
                                     bias=chan[:, 0:1]).then_inc(u_rootc.sem, 1)
                for k in range(nb):
                    if not (isinstance(G.g, int) and G.g == 0):
                        act.wait_ge(u_hw[k], G.g * 16)
                    act.wait_ge(u_h0.sem, u_h0.after(G.g * GB + k))
                    nc.scalar.copy(hs[:, k, 0:R * C // 2], bank[6][:, :]).then_inc(u_hc0.sem, 1)
                    act.wait_ge(u_h1.sem, u_h1.after(G.g * GB + k))
                    nc.scalar.copy(hs[:, k, R * C // 2:], bank[7][:, :]).then_inc(u_hc1.sem, 1)

            def deviation(G):
                act.wait_ge(u_var.sem, u_var.after(G.g))
                nc.scalar.activation(sd[:, 0:G.nb], vare[:, 0:G.nb], ACT.Sqrt).then_inc(u_sd.sem, 1)

            def between(G):
                relations(G)
                if not G.tail:
                    deviation(Group(G.pair, G.b + 1))
            update(Group(0, 0))
            deviation(Group(0, 0))
            skewed(act, lambda G: None if G.first and G.b == 0 else update(G), between)
            edge_loop(1)

            act.wait_ge(s_bv, 1)
            nc.scalar.activation(baff[:, 1:2], baff[:, 0:1], ACT.Sqrt).then_inc(s_bsd, 1)
            act.wait_ge(s_aff, 1)

            def exponential(G):
                b, nb = G.b, G.nb
                act.wait_ge(f_m.sem, f_m.after(G.g - 2))
                act.sem_inc(gm, 1)
                nc.scalar.activation(zb[:, b, 0:nb, :], agg[:, bass.ds(G.g * (GB * P), nb * P)].rearrange("p (k c) -> p k c", c=P),
                                     ACT.Identity, bias=baff[:, 4:5], scale=baff[:, 3:4]).then_inc(f_z.sem, 1)
                act.wait_ge(f_cap.sem, f_cap.after(G.g))
                nc.scalar.activation(ez[:, b, 0:nb, :], cap[:, b, 0:nb, :], ACT.Exp).then_inc(f_exp.sem, 1)
                act.wait_ge(f_u.sem, f_u.after(G.g))
                nc.scalar.activation(cap[:, b, 0:nb, :], ez[:, b, 0:nb, :], ACT.Copy, bias=2.0).then_inc(f_d.sem, 1)
            groups(act, exponential)
            act.wait_ge(s_fv, 1)
            nc.scalar.activation(sdall[:, 1, :], sdall[:, 0, :], ACT.Sqrt).then_inc(s_fsd, 1)
            act.wait_ge(s_scale, 1)

            def normalise(G):
                if G.tail:
                    return
                if not G.first:
                    act.wait_ge(f_o[G.b], G.pair * 16)
                    act.sem_inc(gm, 1)
                for k in range(1, GB, 2):
                    n = G.g * GB + k
                    ins = nc.scalar.activation(xs[:, G.b, k, :].unsqueeze(1), x1[:, bass.ds(n, 1), :], ACT.Identity,
                                               bias=sdall[:, 0, bass.ds(n, 1)], scale=sdall[:, 2, bass.ds(n, 1)])
                ins.then_inc(f_n1.sem, 1)
            groups(act, normalise)

        @block.vector
        def _(dve):
            v = nc.vector
            for k, pad in enumerate((0, FAR, 0)):
                v.memset(raw[:, k, CH - 1, :], pad).then_inc(s_pad, 1)
            v.memset(raw_w[:, CH - 1, :], 0.0).then_inc(s_pad, 1)
            v.memset(cnt_odd[0:P // 2, 0, :], 0.0).then_inc(s_clear, 1)
            v.memset(inv_win[P // 2:P, BLOCKS - 1, 1, :, :], 0.0).then_inc(s_clear, 1)
            v.memset(tgt_win[P // 2:P, BLOCKS - 1, 1, :, :], 0.0).then_inc(s_clear, 1)
            dve.wait_ge(s_edges, 16 * 12)
            for k in range(3):
                v.tensor_copy(rawf[:, k, :, :], raw[:, k, :, :]).then_inc(s_cast, 1)
            dve.wait_ge(s_ecp, 8)
            ch = Chain(dve, c_edge)
            for o, n in ((0, TILES), (TILES, BODY_T)):
                ch.step(v.tensor_copy(idx[0][:, o:o + n], src_f[:, 0:n]))
                ch.step(v.scalar_tensor_tensor(out=idx[1][:, o:o + n], in0=src_f[:, 0:n], scalar=float(R),
                                               in1=type_f[:, 0:n], op0=ALU.mult, op1=ALU.add))
            ch.step(v.tensor_copy(first_i, dst_f[0:1, 0:TILES:QT]))
            ch.step(v.tensor_scalar(win_tab[0:1, 0:QUADS], first_i, 6, None, ALU.arith_shift_right))
            v.tensor_scalar(win_f, win_tab[0:1, 0:QUADS], 64.0, None, ALU.mult).then_inc(s_base, 1)
            dve.wait_ge(s_baseb, 1)
            ch.step(v.tensor_tensor(rel0[:, :].rearrange("p (q j) -> p q j", j=QT),
                                    dst_f[:, 0:TILES].rearrange("p (q j) -> p q j", j=QT),
                                    bank[0][:, 0:QUADS].unsqueeze(2).broadcast_to([P, QUADS, QT]), ALU.subtract))
            ch.step(v.tensor_scalar(outside[:, :], rel0[:, :], 0.0, None, ALU.is_ge))
            ch.step(v.scalar_tensor_tensor(out=inside, in0=rel0[:, :], scalar=float(P), in1=outside[:, :],
                                           op0=ALU.is_lt, op1=ALU.mult))
            ch.step(v.scalar_tensor_tensor(out=outside[:, :], in0=dst_f[:, 0:TILES], scalar=float(FAR // 2), in1=inside,
                                           op0=ALU.is_lt, op1=ALU.subtract))
            v.reduce_sum(n_far[:, :], outside[:, :], AX.X).then_inc(s_nfar, 1)
            ch.step(v.scalar_tensor_tensor(out=far0[:, :], in0=dst_f[:, 0:TILES], scalar=float(FAR), in1=outside[:, :],
                                           op0=ALU.add, op1=ALU.mult))
            ch.step(v.tensor_scalar(far0[:, :], far0[:, :], float(-FAR), None, ALU.add))
            dve.wait_ge(s_nfars, 1)
            ch.step(v.tensor_scalar(passes_f[:, 0:1], bank[1][0:1, 0:1], 1.0, float(BLOCKS), ALU.min, ALU.mult))
            v.tensor_scalar(passes_i[:, :], passes_f[:, 0:1], 1.0, None, ALU.add).then_inc(s_tab, 1)
            start_credits(dve, bc, u_st, u_y, u_var, u_x1, f_cap, f_u, f_r, f_y, f_n)
            pool_credits = (u_x1k,)
            start_credits(dve, *pool_credits)
            dve.wait_ge(s_w, 16 * 11)

            def prepare(G):
                nb = G.nb
                ch = Chain(dve, c_prep, G.g * 6)
                if G.tail:
                    dve.wait_ge(xtr.sem, xtr.after(GROUPS - 2))
                    v.memset(xs[LAST // 32 * 32:, 0, 0, :], 0.0).then_inc(s_tail, 1)
                dve.wait_ge(abm.sem, abm.after(G.g))
                part = bsum[:, 0:nb, :]
                ins = v.tensor_tensor(part, bank[4 + G.b][:, 0:nb * P].rearrange("p (k c) -> p k c", c=C), over(bmsg, nb), ALU.add)
                ch.step(ins)
                dve.sem_inc(bc.sem, 1)
                ch.step(v.tensor_copy(b3[:, 0:nb, 0, :], part))
                ch.step(v.tensor_tensor(bres[:, 0:nb, :], part, b3[:, 0:nb, 0, :], ALU.subtract))
                ch.step(v.tensor_copy(b3[:, 0:nb, 1, :], bres[:, 0:nb, :]))
                ch.step(v.tensor_tensor(b3[:, 0:nb, 2, :], bres[:, 0:nb, :], b3[:, 0:nb, 1, :], ALU.subtract))
                ch.step(v.tensor_copy(tgt_win[:, bass.ds(G.g * GB, nb), 0, :, :].rearrange("p q k c -> p q (k c)"),
                                      b3[:, 0:nb, :, :].rearrange("p q k c -> p q (k c)")))
            groups(dve, prepare)

            def edge_loop(k):
                l = L[k]
                start_credits(dve, *(l[s] for s in ("onehot_ready", "lookup_used", "picked_ready", "window_added", "counts_added")),
                              *([l["used"]] if not k else []))
                v.tensor_copy(rel[:, :], rel0[:, :]).then_inc(l["targets"], 1)
                v.tensor_copy(idx_stage[:, :, :], idx[k][:, 0:BODY_T].rearrange("p (h c) -> p h c", h=2)).then_inc(l["staged"], 2)
                passes = dve.value_load(passes_i[0:1, 0:1], min_val=1, max_val=PASSES)
                with dve.Fori(0, passes) as p:
                    at, step = pass_values(dve, p)
                    dve.wait_ge(l["targets"], p + 1)
                    dve.sem_inc(gm, 1)
                    with dve.Fori(0, ITERS) as i:
                        it = dve.snap(p * ITERS + i)
                        n0 = dve.snap(it * SLOTS)

                        def one_hot(s):
                            b, n = s % 4, n0 + s
                            col = i * BODY_T + s * QT
                            dve.wait_ge(l["scattered"].sem, l["scattered"].after(n - 4))
                            for j in range(QT):
                                v.tensor_scalar(onehot[:, b, j, :], node_iota[:, :], rel[:, bass.ds(col + j, 1)], None, ALU.is_equal)
                            ins = v.tensor_tensor(
                                types[:, b, :, :], node_iota[:, 0:R].unsqueeze(1).broadcast_to([P, QT, R]),
                                type_f[:, bass.ds(col, QT)].unsqueeze(2).broadcast_to([P, QT, R]), ALU.is_equal)
                            ins.then_inc(l["onehot_ready"].sem, 1)

                        def weigh(s):
                            b, n = s % 2, n0 + s
                            dve.wait_ge(l["messages_ready"].sem, l["messages_ready"].after(n - 2))
                            dve.wait_ge(l["gathered"][s], (it + 1) * (16 * QT))
                            for j in range(QT):
                                ins = v.scalar_tensor_tensor(
                                    out=pre[:, b, j, :], in0=w_dist[:, :], scalar=dist[:, bass.ds(i * BODY_T + (s * QT + j), 1)],
                                    in1=rows[:, s, j, :], op0=ALU.mult, op1=ALU.add)
                            ins.then_inc(l["used"].sem, 1)

                        def use_lookup(s):
                            b, n = s % 2, n0 + s
                            dve.wait_ge(l["looked_up"].sem, l["looked_up"].after(n))
                            if k == 0:
                                dve.wait_ge(l["used"].sem, l["used"].after(n))
                                v.tensor_tensor(pre[:, b, :, :], pre[:, b, :, :], bank[2 + b][:, :].rearrange("p (k c) -> p k c", c=C),
                                                ALU.add).then_inc(l["lookup_used"].sem, 1)
                            else:
                                dve.wait_ge(l["messages_ready"].sem, l["messages_ready"].after(n - 2))
                                dve.wait_ge(l["lookup_used"].sem, l["lookup_used"].after(n - 1))
                                v.tensor_tensor(picked[:, :, :, :], bank[2 + b][:, 0:QT * 3 * R].rearrange("p (j h r) -> p j h r", j=QT, h=3),
                                                types[:, s % 4, :, :].unsqueeze(2).broadcast_to([P, QT, 3, R]), ALU.mult
                                                ).then_inc(l["picked_ready"].sem, 1)
                                dve.wait_ge(l["picked_ready"].sem, l["picked_ready"].after(n))
                                v.reduce_sum(edge_w[:, b, :], picked[:, :, :, :].rearrange("p j h r -> p j (h r)"), AX.X).then_inc(l["lookup_used"].sem, 1)

                        def add_window(s):
                            b, n = s % 2, n0 + s
                            w = window_of(dve, i, s, at, step)
                            node = dve.snap(w * (P // 2))
                            dve.wait_ge(l["scattered"].sem, l["scattered"].after(n))
                            dve.wait_ge(l["window_added"].sem, l["window_added"].after(n - 1))
                            v.tensor_tensor(agg[:, bass.ds(node, P)], agg[:, bass.ds(node, P)], bank[4 + b][:, 0:P], ALU.add
                                            ).then_inc(l["window_added"].sem, 1)
                            if k == 0:
                                dve.wait_ge(l["counts_added"].sem, l["counts_added"].after(n - 1))
                                v.tensor_tensor(cnt[:, bass.ds(w, 1), :], cnt[:, bass.ds(w, 1), :], bank[6 + b][:, 0:R].unsqueeze(1), ALU.add
                                                ).then_inc(l["counts_added"].sem, 1)

                        def restage(h):
                            dve.wait_ge(l["messages_ready"].sem, l["messages_ready"].after(n0 + (h * HALF + HALF - 1)))
                            v.tensor_scalar(idx_stage[:, h, :], idx[k][:, bass.ds(i * BODY_T + (h * STAGE_T + BODY_T), STAGE_T)],
                                            0.0, None, ALU.add).then_inc(l["staged"], 1)

                        one_hot(0)
                        one_hot(1)
                        for s in range(SLOTS):
                            if k == 0:
                                weigh(s)
                            if s + 2 < SLOTS:
                                one_hot(s + 2)
                            use_lookup(s)
                            if s >= 1:
                                add_window(s - 1)
                            if s == HALF:
                                restage(0)
                        add_window(SLOTS - 1)
                        restage(1)
                    dve.wait_ge(l["onehot_ready"].sem, l["onehot_ready"].after((p + 1) * QUADS - 1))
                    v.tensor_scalar(rel[:, :], far0[:, :], moved[:, bass.ds(p, 1)], None, ALU.subtract).then_inc(l["targets"], 1)
                end = passes * QUADS - 1
                dve.wait_ge(l["window_added"].sem, l["window_added"].after(end))
                if k == 0:
                    dve.wait_ge(l["counts_added"].sem, l["counts_added"].after(end))
                dve.sem_inc(l_done[k], 1)

            dve.wait_ge(s_clear, 5)
            edge_loop(0)

            ch = Chain(dve, c_inv)
            dve.wait_ge(s_oddc, 32)
            even = cnt[:, :, :].rearrange("p (q h) r -> p q h r", h=2)[:, :, 0, :]
            ch.step(v.tensor_tensor(inv[:, :, :], even, cnt_odd[:, :, :], ALU.add))
            ch.step(v.tensor_scalar(cnt_odd[:, :, :], inv[:, :, :], 1.0, None, ALU.max))
            ch.step(v.reciprocal(inv[:, :, :], cnt_odd[:, :, :]))
            ch.step(v.tensor_copy(inv3[:, :, 0, :], inv[:, :, :]))
            ch.step(v.tensor_tensor(cnt_odd[:, :, :], inv[:, :, :], inv3[:, :, 0, :], ALU.subtract))
            ch.step(v.tensor_copy(inv3[:, :, 1, :], cnt_odd[:, :, :]))
            v.tensor_tensor(inv3[:, :, 2, :], cnt_odd[:, :, :], inv3[:, :, 1, :], ALU.subtract).then_inc(s_inv, 1)

            def norm_statistics(ch, values, nb):
                for k in range(nb):
                    ins = v.bn_stats(st6[:, k, :], values(k))
                ch.step(ins)
                dve.sem_inc(gm, 1)
                for k in range(nb):
                    ins = v.bn_aggr(mv[:, k, :], st6[:, k, :])
                ch.step(ins)

            def stage_sums(G):
                b, nb = G.b, G.nb
                if G.tail:
                    dve.wait_ge(u_y.sem, u_y.after(GROUPS - 2))
                    v.memset(xs[LAST // 32 * 32:, 0, 0, :], 0.0).then_inc(s_tail, 1)
                dve.wait_ge(u_mm.sem, u_mm.after(G.g - 2))
                v.tensor_scalar(aT[:, b, 0:nb, :], agg[:, bass.ds(G.g * (GB * P), nb * P)].rearrange("p (k c) -> p k c", c=P),
                                1.0, None, ALU.mult).then_inc(u_st.sem, 1)

            def update(G):
                b, nb = G.b, G.nb
                ch = Chain(dve, c_upd, G.g * UPD_STEPS)
                dve.wait_ge(u_mm.sem, u_mm.after(G.g))
                dve.wait_ge(ul[b], G.pair * 16 + 16)
                yy, y1 = y[:, 0:nb, :], y2[:, 0:nb, :]
                ch.step(v.tensor_tensor(y1, bank[3][:, 0:nb * P].rearrange("p (k c) -> p k c", c=C), over(bupd, nb), ALU.add))
                ch.step(v.scalar_tensor_tensor(out=yy, in0=y1, scalar=0.0, in1=bank[2][:, 0:nb * P].rearrange("p (k c) -> p k c", c=C),
                                               op0=ALU.max, op1=ALU.add))
                ch.step(v.tensor_tensor(yy, yy, xs[:, b, 0:nb, :], ALU.add))
                dve.sem_inc(u_y.sem, 1)
                norm_statistics(ch, lambda k: y[:, k, :], nb)
                v.tensor_scalar(vare[:, 0:nb], mv[:, 0:nb, 1], EPS, None, ALU.add).then_inc(u_var.sem, 1)
                dve.wait_ge(u_sd.sem, u_sd.after(G.g))
                ch.step(v.reciprocal(rstd[:, 0:nb], sd[:, 0:nb]))
                dve.wait_ge(u_x1k.sem, u_x1k.after(G.g - 2))
                dve.wait_ge(u_t1.sem, u_t1.after(G.g - 2))
                for k in range(nb):
                    ins = v.tensor_scalar(x1s[:, b, k, :], y[:, k, :], mv[:, k, 0:1], rstd[:, k:k + 1], ALU.subtract, ALU.mult)
                ch.step(ins)
                dve.sem_inc(u_x1.sem, 1)

            skewed(dve, stage_sums, update)
            dve.wait_ge(u_rootc.sem, u_rootc.after(GROUPS))
            dve.wait_ge(u_x1k.sem, u_x1k.after(GROUPS))
            edge_loop(1)

            ch = Chain(dve, c_fin)
            for c in range(NST):
                ins = v.bn_stats(bst[:, c, :], agg[:, c * SC:(c + 1) * SC])
            ch.step(ins)
            ch.step(v.bn_aggr(bmv[:, :], bst[:, :, :].rearrange("p a b -> p (a b)")))
            v.tensor_scalar(baff[:, 0:1], bmv[:, 1:2], EPS, None, ALU.add).then_inc(s_bv, 1)
            dve.wait_ge(s_bsd, 1)
            ch.step(v.reciprocal(baff[:, 2:3], baff[:, 1:2]))
            ch.step(v.tensor_tensor(baff[:, 3:4], baff[:, 2:3], chan[:, 1:2], ALU.mult))
            ch.step(v.tensor_tensor(baff[:, 5:6], bmv[:, 0:1], baff[:, 3:4], ALU.mult))
            v.tensor_tensor(baff[:, 4:5], chan[:, 2:3], baff[:, 5:6], ALU.subtract).then_inc(s_aff, 1)
            start = ch.n

            def mish(G):
                b, nb = G.b, G.nb
                z, e, c = zb[:, b, 0:nb, :], ez[:, b, 0:nb, :], cap[:, b, 0:nb, :]
                dve.wait_ge(f_z.sem, f_z.after(G.g))
                dve.wait_ge(f_tr.sem, f_tr.after(G.g - 2))
                v.tensor_scalar(c, z, EXP_CAP, None, ALU.min).then_inc(f_cap.sem, 1)
                dve.wait_ge(f_exp.sem, f_exp.after(G.g))
                v.scalar_tensor_tensor(out=e, in0=e, scalar=2.0, in1=e, op0=ALU.add, op1=ALU.mult).then_inc(f_u.sem, 1)
                dve.wait_ge(f_d.sem, f_d.after(G.g))
                v.reciprocal(c, c).then_inc(f_r.sem, 1)

            def final_rows(G):
                b, nb = G.b, G.nb
                ch = Chain(dve, c_fin, G.g * 3 + start)
                dve.wait_ge(f_tr.sem, f_tr.after(G.g))
                at = bass.ds(G.g * GB, nb)
                v.tensor_tensor(x1[:, at, :], x1[:, at, :], bank[b][:, 0:nb * P].rearrange("p (k c) -> p k c", c=C), ALU.add
                                ).then_inc(f_y.sem, 1)
                dve.wait_ge(f_y.sem, f_y.after(G.g))
                dve.sem_inc(gm, 1)
                norm_statistics(ch, lambda k: x1[:, bass.ds(G.g * GB + k, 1), :], nb)
                ch.step(v.tensor_scalar(mvall[:, at, :], mv[:, 0:nb, :], 1.0, None, ALU.mult))
            skewed(dve, mish, final_rows)
            v.tensor_scalar(sdall[:, 0, :], mvall[:, :, 1], EPS, None, ALU.add).then_inc(s_fv, 1)
            dve.wait_ge(s_fsd, 1)
            ch = Chain(dve, c_nrm)
            ch.step(v.reciprocal(sdall[:, 2, :], sdall[:, 1, :]))

            ch.step(v.scalar_tensor_tensor(out=sdall[:, 0, :], in0=mvall[:, :, 0], scalar=-1.0, in1=sdall[:, 2, :],
                                           op0=ALU.mult, op1=ALU.mult))
            dve.sem_inc(s_scale, 1)

            def normalise(G):
                if not G.first:
                    dve.wait_ge(f_o[G.b], G.pair * 16)
                for k in range(0, G.nb, 2):
                    n = G.g * GB + k
                    ins = v.tensor_scalar(xs[:, G.b, k, :].unsqueeze(1), x1[:, bass.ds(n, 1), :], mvall[:, bass.ds(n, 1), 0],
                                          sdall[:, 2, bass.ds(n, 1)], ALU.subtract, ALU.mult)
                ins.then_inc(f_n.sem, 1)
            groups(dve, normalise)


_INS = ["x", "src", "dst", "edge_type_8", "edge_weight1", "L0_gnn_W_res", "L0_gnn_W_msg", "L0_gnn_b_msg", "L0_gnn_W_upd",
        "L0_gnn_b_upd", "L1_gnn_W", "L1_gnn_root", "L1_gnn_bias", "L1_gnn_gamma", "L1_gnn_beta"]


def kernel(**inputs):
    import numpy as _np
    import concourse.bacc as _bacc
    from concourse import mybir as _mybir
    from concourse.bass_utils import run_bass_kernel_spmd as _run

    nc = _bacc.Bacc("TRN2", target_bir_lowering=False, num_devices=1)
    arrays, args = {}, []
    for name in _INS:
        a = _np.ascontiguousarray(inputs[name])
        arrays[f"in_{name}_dram"] = a
        args.append(nc.dram_tensor(f"in_{name}_dram", a.shape, _mybir.dt.from_np(a.dtype), kind="ExternalInput").ap())
    args.append(nc.dram_tensor("out_0_dram", inputs["x"].shape, _mybir.dt.float32, kind="ExternalOutput").ap())
    bass_gnn(nc, *args)
    r = _run(nc, [arrays], core_ids=[0])
    return r.results[0]["out_0_dram"]
```

```python
from contextlib import ExitStack

import concourse.bass as bass
from concourse import mybir

ALU = mybir.AluOpType
ACT = mybir.ActivationFunctionType
AX = mybir.AxisListType
F32 = mybir.dt.float32
BF16 = mybir.dt.bfloat16
I32 = mybir.dt.int32

P = 128
QT = 4
SLOTS = 8
HALF = SLOTS // 2
EPS = 1e-5
FAR = 1 << 20
EXP_CAP = 20.0


class Stage:

    def __init__(self, sem, credit=2):
        self.sem, self.credit = sem, credit

    def after(self, n):
        return n + (1 + self.credit)


def bass_gnn(nc, x, src, dst, edge_type, edge_weight, w_res, w_msg, b_msg, w_upd, b_upd,
             w_rel, w_root, b_rel, gamma, beta, out):
    N, C = x.shape
    E = src.shape[0]
    R = w_rel.shape[0]
    assert C == P
    BLOCKS = -(-N // P)
    LAST = N - (BLOCKS - 1) * P
    QUADS = -(-E // (P * QT * SLOTS)) * SLOTS
    TILES = QUADS * QT
    ITERS = QUADS // SLOTS
    CH = -(-TILES // P)
    COLS = CH * P
    GB = 4
    GROUPS = BLOCKS // GB
    assert BLOCKS % GB == 1 and GROUPS % 2 == 0 and (QUADS - 1) * QT * P < E
    FULL = E // P
    NW = (BLOCKS + 1) * P
    PASSES = 1 + BLOCKS
    PAIRS = BLOCKS // 2
    assert PAIRS <= ITERS and BLOCKS % 2 == 1
    BODY_T = SLOTS * QT
    STAGE_T = HALF * QT
    SC = max(d for d in range(1, 513) if N % d == 0)
    NST = N // SC
    PREP_STEPS = 4
    UPD_STEPS = 8

    src_rows = nc.dram_tensor("src_rows", (BLOCKS * P, C), F32).ap()
    upd_rows = nc.dram_tensor("upd_rows", (BLOCKS * P, 2, C), F32).ap()
    rel_rows = nc.dram_tensor("rel_rows", (BLOCKS * P * R, C), F32).ap()

    ctx = ExitStack()
    with ctx:
        def sb(name, shape, dt=F32):
            return ctx.enter_context(nc.sbuf_tensor(name, shape, dt))

        def sem(name):
            return ctx.enter_context(nc.semaphore(name))

        bank = [ctx.enter_context(nc.psum_tensor(f"bank{i}", [P, 512], F32)) for i in range(8)]

        ident = sb("ident", [P, P])
        node_iota = sb("node_iota", [P, P])
        ones = sb("ones", [P, P])
        w_ab = sb("w_ab", [P, 2, C])
        w_dist = sb("w_dist", [P, C])
        w_self = sb("w_self", [P, C])
        w_up = sb("w_up", [P, 2, C])
        w_r = sb("w_r", [P, R, C])
        w_ro = sb("w_ro", [P, C])
        bmsg = sb("bmsg", [P, C])
        bupd = sb("bupd", [P, C])
        chan = sb("chan", [P, 3])
        onehot = sb("onehot", [P, 4, QT, P])
        onehot_mem = onehot[:, :, :, :].rearrange("p b j c -> p (b j c)")
        src_f = onehot_mem[:, 0:COLS]
        dst_f = onehot_mem[:, COLS:2 * COLS]
        type_f = sb("type_f", [P, COLS])
        dist = sb("dist", [P, COLS])
        idx = [sb(f"idx{k}", [P, TILES + BODY_T], I32) for k in range(2)]
        idx_stage = sb("idx_stage", [P, 2, STAGE_T], I32)
        rel0 = sb("rel0", [P, TILES])
        far0 = sb("far0", [P, TILES])
        rel = sb("rel", [P, TILES])
        inside = src_f[:, 0:TILES]
        moved = sb("moved", [P, PASSES])
        outside = rel
        n_far = sb("n_far", [P, 1])
        passes_f = sb("passes_f", [1, 1])
        passes_i = sb("passes_i", [1, 1], I32)
        win_tab = sb("win_tab", [1, 2 * QUADS + BLOCKS], I32)
        pair_tab = sb("pair_tab", [1, ITERS], I32)
        pass_tab = sb("pass_tab", [1, 2, PASSES], I32)
        win_mem = sb("win_mem", [P, BLOCKS * 3 * C])
        tgt_win = win_mem[:, :].bitcast(BF16).rearrange("p (q h k c) -> p q h k c", h=2, k=3, c=C)
        x1 = win_mem[:, 0:BLOCKS * C].rearrange("p (q c) -> p q c", c=C)
        inv_win = sb("inv_win", [P, BLOCKS, 2, 3, R], BF16)
        agg = sb("agg", [P, NW])
        raw = agg[:, 0:3 * COLS].bitcast(I32).rearrange("p (k c e) -> p k c e", k=3, e=P)
        raw_w = agg[:, 3 * COLS:4 * COLS].rearrange("p (c e) -> p c e", e=P)
        rawf = agg[:, 4 * COLS:7 * COLS].rearrange("p (k c e) -> p k c e", k=3, e=P)
        cnt = sb("cnt", [P, 2 * BLOCKS, R])
        rows = sb("rows", [P, SLOTS, QT, C])
        onehot_t = sb("onehot_t", [P, 2, QT, P], BF16)
        types = sb("types", [P, 4, QT, R])
        pre = sb("pre", [P, 2, QT, C])
        msg = sb("msg", [P, 2, QT, C])
        picked = sb("picked", [P, QT, 3, R])
        edge_w = sb("edge_w", [P, 2, QT])
        first_i = rows[0:1, 6, :, :].rearrange("p a b -> p (a b)")[:, 0:QUADS].bitcast(I32)
        win_f = rows[0:1, 7, :, :].rearrange("p a b -> p (a b)")[:, 0:QUADS]
        xs = rows[:, 0:2, :, :]
        xT = rows[:, 2:4, :, :]
        a_out = rows[:, 4:6, :, :]
        hs = sb("hs", [P, GB, R * C])
        pair_x = hs[:, 0, 0:2 * C].rearrange("p (k c) -> p k c", k=2)
        pair_xT = hs[:, 1, 0:2 * P].rearrange("p (k c) -> p k c", k=2)
        upd_out = hs[:, 2, 0:4 * C].rearrange("p (k u c) -> p k u c", k=2, u=2)
        upd_in = rows[:, 2:6, :, :].rearrange("p s j c -> p (s j c)").rearrange("p (b k u c) -> p b k u c", b=2, k=GB, u=2)
        bsum = msg[:, 0, :, :]
        bres = pre
        x_tail = sb("x_tail", [P, C])
        x1s = onehot[:, 0:2, :, :]
        aT = pre
        x1T = sb("x1T", [P, GB, P])
        y2 = msg[:, 0, :, :]
        y = msg[:, 1, :, :]
        st6 = sb("st6", [P, GB, 6])
        mv = sb("mv", [P, GB, 2])
        vare = sb("vare", [P, GB])
        sd = sb("sd", [P, GB])
        rstd = sb("rstd", [P, GB])
        cnt_odd = sb("cnt_odd", [P, BLOCKS, R])
        inv = sb("inv", [P, BLOCKS, R])
        inv3 = inv_win[:, :, 0, :, :]
        zb, ez, cap = pre, onehot[:, 0:2, :, :], msg
        mish_out = hs[:, 0:2, :].rearrange("p b (k c) -> p b k c", c=C)
        bst = sb("bst", [P, NST, 6])
        bmv = sb("bmv", [P, 2])
        baff = sb("baff", [P, 6])
        mvall = sb("mvall", [P, BLOCKS, 2])
        sdall = far0[:, 0:3 * BLOCKS].rearrange("p (k q) -> p k q", k=3)

        s_wab, s_wup = sem("message_weights_loaded"), sem("update_weights_loaded")
        s_bm, s_w2 = sem("message_bias_loaded"), sem("other_weights_loaded")
        s_const, s_pad, s_edges = sem("constants_set"), sem("edge_padding_set"), sem("edges_loaded")
        s_cast, s_etr, s_ecp = sem("edges_cast"), sem("edges_transposed"), sem("edges_copied")
        s_base, s_baseb = sem("window_starts_ready"), sem("window_starts_spread")
        s_nfar, s_nfars, s_tab = sem("far_edges_counted"), sem("far_edges_summed"), sem("tables_ready")
        s_clear = sem("sums_cleared")
        s_tail, s_xtail = sem("tail_rows_zeroed"), sem("tail_x_loaded")
        gm = sem("waits_taken")
        c_edge, c_far, c_prep, c_upd, c_idx, c_fin, c_nrm = (sem(f"chain_{n}") for n in (
            "edges", "far_edges", "prepare", "update", "indices", "final", "norm"))
        xl = [sem(f"x_loaded{i}") for i in range(2)]
        aw = [sem(f"source_part_written{i}") for i in range(2)]
        xtr, xtc, abm, ac, bc, rests, thirds = (Stage(sem(n)) for n in (
            "x_transposed", "x_transpose_copied", "parts_multiplied", "source_part_copied", "target_part_read",
            "target_rests_ready", "target_thirds_ready"))
        s_tup, s_tupc = sem("tail_products_ready"), sem("tail_products_copied")
        p_l, p_w = sem("pair_x_loaded"), sem("products_written")
        p_tr, p_tc, p_mm, p_c = (Stage(sem(n)) for n in (
            "pair_x_transposed", "pair_x_copied", "pair_multiplied", "pair_products_copied"))
        s_odd = sem("odd_windows_ready")
        s_oddc, c_inv, s_inv, s_oddi = sem("odd_counts_moved"), sem("chain_inverse"), sem("inverse_ready"), sem("odd_inverse_ready")
        L = [dict(
            staged=sem(f"indices_staged{k}"),
            gathered=[sem(f"gathered{k}_{s}") for s in range(SLOTS)],
            issued=sem(f"quads_issued{k}"),
            targets=sem(f"targets_ready{k}"),
            used=Stage(sem(f"rows_used{k}"), SLOTS),
            **{n: Stage(sem(f"{n}{k}")) for n in (
                "onehot_ready", "onehot_turned", "turned_copied", "looked_up", "lookup_used",
                "picked_ready", "messages_ready", "window_added", "counts_added")},
            scattered=Stage(sem(f"scattered{k}"), 4),
        ) for k in range(2)]
        l_done = [sem(f"layer_summed{k}") for k in range(2)]
        ul = [sem(f"update_x_loaded{i}") for i in range(2)]
        url = [sem(f"update_parts_loaded{i}") for i in range(2)]
        u_hw = [sem(f"relation_rows_written{k}") for k in range(GB)]
        (u_st, u_mm, u_y, u_var, u_sd, u_x1, u_x1k, u_t1, u_t1c, u_root, u_rootc, u_h0, u_h1, u_hc0, u_hc1) = (Stage(sem(n)) for n in (
            "sums_staged", "update_multiplied", "update_y_ready",
            "update_variance_ready", "update_deviation_ready", "x1_ready", "x1_kept", "x1_transposed", "x1_transpose_copied",
            "root_multiplied", "root_added", "relations_low_multiplied", "relations_high_multiplied",
            "relations_low_copied", "relations_high_copied"))
        s_bv, s_bsd, s_aff = sem("batch_variance_ready"), sem("batch_deviation_ready"), sem("batch_affine_ready")
        f_z, f_cap, f_exp, f_u, f_d, f_r, f_t, f_m, f_tr, f_y = (Stage(sem(n)) for n in (
            "final_z_ready", "final_capped", "final_exp_ready", "final_u_ready", "final_divisor_ready", "final_reciprocal_ready",
            "final_ratio_ready", "final_mish_ready", "final_rows_ready", "final_rows_kept"))
        s_fv, s_fsd = sem("final_variances_ready"), sem("final_deviations_ready")
        s_scale = sem("final_scales_ready")
        f_n, f_n1 = Stage(sem("final_normalised_even")), Stage(sem("final_normalised_odd"))
        f_o = sem("final_written")

        x_groups = x[0:GROUPS * GB * P, :].rearrange("(q p) c -> p q c", p=P)
        src_groups = src_rows[0:GROUPS * GB * P, :].rearrange("(q p) c -> p q c", p=P)
        x_blocks = x[0:PAIRS * 2 * P, :].rearrange("(q p) c -> p q c", p=P)
        upd_blocks = upd_rows[0:PAIRS * 2 * P, :, :].rearrange("(q p) u c -> p q u c", p=P)
        upd_groups = upd_rows[0:GROUPS * GB * P, :, :].rearrange("(q p) u c -> p q u c", p=P)
        out_groups = out[0:GROUPS * GB * P, :].rearrange("(q p) c -> p q c", p=P)
        rel_blocks = rel_rows.rearrange("(q p r) c -> p q (r c)", p=P, r=R)

        class Group:

            def __init__(self, pair, b):
                self.pair, self.b, self.g = pair + b // 2, b % 2, pair * 2 + b
                self.first = isinstance(self.g, int) and self.g < 2
                self.tail = isinstance(self.g, int) and self.g == GROUPS
                self.beyond = isinstance(self.g, int) and self.g + 2 > GROUPS
                self.nb = 1 if self.tail else GB

        def groups(eng, step):
            step(Group(0, 0))
            step(Group(0, 1))
            with eng.Fori(1, GROUPS // 2) as i:
                step(Group(i, 0))
                step(Group(i, 1))
            step(Group(GROUPS // 2, 0))

        def skewed(eng, a, b, lead=1):
            for k in range(lead):
                a(Group(0, k))
            for k in range(2):
                a(Group(0, k + lead))
                b(Group(0, k))
            with eng.Fori(1, GROUPS // 2 - 1) as i:
                for k in range(2):
                    a(Group(i, k + lead))
                    b(Group(i, k))
            for k in range(3):
                if k + lead <= 2:
                    a(Group(GROUPS // 2 - 1, k + lead))
                b(Group(GROUPS // 2 - 1, k))

        class Chain:

            def __init__(self, eng, s, base=0):
                self.eng, self.s, self.base, self.n = eng, s, base, 0

            def step(self, ins):
                self.n += 1
                ins.then_inc(self.s, 1)
                self.eng.wait_ge(self.s, self.base + self.n)

        def third_of(G, h):
            return tgt_win[:, bass.ds(G.g * GB, G.nb), 0, h, :]

        def x_block(G, k):
            return x_tail[:, :] if G.tail else xs[:, G.b, k, :]

        def over(v, nb):
            return v[:, :].unsqueeze(1).broadcast_to([P, nb, C])

        def start_credits(eng, *stages):
            for s in stages:
                eng.sem_inc(s.sem, s.credit)

        def pass_values(eng, p):
            at = eng.value_load(pass_tab[0:1, 0, bass.ds(p, 1)], min_val=0, max_val=QUADS + BLOCKS - 1)
            step = eng.value_load(pass_tab[0:1, 1, bass.ds(p, 1)], min_val=0, max_val=1)
            return at, step

        def window_of(eng, i, s, at, step):
            return eng.value_load(win_tab[0:1, bass.ds(at + (i * SLOTS + s) * step, 1)], min_val=0, max_val=2 * BLOCKS - 1)

        block = ctx.enter_context(nc.Block())

        @block.sync
        def _(sp):
            first = (FULL // P) * P * P
            full = (FULL % P) * P
            sp.wait_ge(s_pad, 4)
            for k, e in enumerate((src, dst, edge_type, edge_weight)):
                d = raw[:, k, :, :] if k < 3 else raw_w
                e = e if k < 3 else e.rearrange("e a -> (e a)")
                sp.dma_start(d[:, 0:FULL // P, :], e[0:first].rearrange("(c p e) -> p c e", p=P, e=P)).then_inc(s_edges, 16)
                sp.dma_start(d[0:FULL % P, FULL // P, :],
                             e[first:first + full].rearrange("(p e) -> p e", e=P)).then_inc(s_edges, 16)
                sp.dma_start(d[FULL % P:FULL % P + 1, FULL // P, 0:E - FULL * P],
                             e[FULL * P:E].rearrange("(p e) -> p e", p=1)).then_inc(s_edges, 16)
            sp.dma_start(w_ab[:, :, :], w_msg[0:2 * C, :].rearrange("(k p) c -> p k c", p=P)).then_inc(s_wab, 16)

            def load_x(G, loaded, used):
                if not G.tail:
                    sp.wait_ge(used.sem, used.after(G.g - 2))
                    sp.dma_start(xs[:, G.b, :, :], x_groups[:, bass.ds(G.g * GB, GB), :]).then_inc(loaded[G.b], 16)

            def load_prepare(G):
                load_x(G, xl, xtr)
                if G.first and G.b == 1:
                    sp.dma_start(w_self[:, :], w_res).then_inc(s_wup, 16)
                    sp.dma_start(w_up[:, :, :], w_upd.rearrange("(k p) c -> p k c", p=P)).then_inc(s_wup, 16)
                    sp.dma_start(bmsg[:, :], b_msg.partition_broadcast(P)).then_inc(s_bm, 16)
                    sp.wait_ge(s_tail, 1)
                    sp.dma_start(x_tail[0:LAST, :], x[GROUPS * GB * P:N, :]).then_inc(s_xtail, 16)
                    sp.dma_start(w_dist[:, :], w_msg[2 * C, :].partition_broadcast(P)).then_inc(s_w2, 16)
                    sp.dma_start(bupd[:, :], b_upd.partition_broadcast(P)).then_inc(s_w2, 16)
                    sp.dma_start(w_r[:, :, :], w_rel.rearrange("r p c -> p r c")).then_inc(s_w2, 16)
                    sp.dma_start(w_ro[:, :], w_root).then_inc(s_w2, 16)
                    for k, v in enumerate((b_rel, gamma, beta)):
                        sp.dma_start(chan[:, k:k + 1], v.rearrange("(p a) -> p a", a=1)).then_inc(s_w2, 16)
            groups(sp, load_prepare)
            sp.wait_ge(s_tupc, 1)
            sp.dma_start(upd_rows[PAIRS * 2 * P:, :, :], upd_out[:, 0, :, :]).then_inc(p_w, 16)
            sp.wait_ge(s_clear, 5)
            sp.wait_ge(thirds.sem, thirds.after(GROUPS))
            sp.wait_ge(aw[0], 16 * (GROUPS // 2 + 1))
            sp.wait_ge(aw[1], 16 * (GROUPS // 2))
            sp.dma_start(tgt_win[0:P // 2, :, 1, :, :], tgt_win[P // 2:P, :, 0, :, :]).then_inc(s_odd, 16)
            sp.dma_start(tgt_win[P // 2:P, 0:BLOCKS - 1, 1, :, :], tgt_win[0:P // 2, 1:BLOCKS, 0, :, :]).then_inc(s_odd, 16)

            sp.wait_ge(s_tab, 1)
            sp.wait_ge(s_const, 12)
            passes = sp.value_load(passes_i[0:1, 0:1], min_val=1, max_val=PASSES)
            with sp.Fori(0, passes) as p:
                with sp.Fori(0, ITERS) as i:
                    it = sp.snap(p * ITERS + i)
                    q = sp.value_load(pair_tab[0:1, bass.ds(i, 1)], min_val=0, max_val=PAIRS * 2 - 2)
                    sp.wait_ge(p_tr.sem, p_tr.after(it - 1))
                    sp.dma_start(pair_x, x_blocks[:, bass.ds(q, 2), :]).then_inc(p_l, 16)
                    sp.wait_ge(p_c.sem, p_c.after(it))
                    sp.dma_start(upd_blocks[:, bass.ds(q, 2), :, :], upd_out).then_inc(p_w, 16)
            sp.wait_ge(p_w, (passes * ITERS + 1) * 16)
            sp.wait_ge(L[0]["used"].sem, L[0]["used"].after(passes * QUADS - (SLOTS - 5)))

            def load_update(G):
                load_x(G, ul, u_y)
                if G.tail:
                    sp.wait_ge(u_y.sem, u_y.after(GROUPS - 2))
                    sp.dma_start(upd_in[:, 0, 0, :, :], upd_rows[GROUPS * GB * P:, :, :]).then_inc(url[0], 16)
                else:
                    sp.dma_start(upd_in[:, G.b, :, :, :], upd_groups[:, bass.ds(G.g * GB, GB), :, :]).then_inc(url[G.b], 16)
                if G.first and G.b == 1:
                    sp.wait_ge(l_done[0], 1)
                    by_block = cnt[:, :, :].rearrange("p (q h) r -> p q h r", h=2)
                    sp.dma_start(cnt_odd[0:P // 2, 1:BLOCKS, :], by_block[P // 2:P, 0:BLOCKS - 1, 1, :]).then_inc(s_oddc, 16)
                    sp.dma_start(cnt_odd[P // 2:P, :, :], by_block[0:P // 2, :, 1, :]).then_inc(s_oddc, 16)

            def write_relations(G):
                for k in range(G.nb):
                    n = G.g * GB + k
                    sp.wait_ge(u_hc0.sem, u_hc0.after(n))
                    sp.wait_ge(u_hc1.sem, u_hc1.after(n))
                    sp.dma_start(rel_blocks[:, bass.ds(n, 1), :], hs[:, k:k + 1, :]).then_inc(u_hw[k], 16)
            skewed(sp, load_update, write_relations, 2)
            sp.wait_ge(s_inv, 1)
            sp.dma_start(inv_win[0:P // 2, :, 1, :, :], inv_win[P // 2:P, :, 0, :, :]).then_inc(s_oddi, 16)
            sp.dma_start(inv_win[P // 2:P, 0:BLOCKS - 1, 1, :, :], inv_win[0:P // 2, 1:BLOCKS, 0, :, :]).then_inc(s_oddi, 16)

            def store(G):
                sp.wait_ge(f_n.sem, f_n.after(G.g))
                if not G.tail:
                    sp.wait_ge(f_n1.sem, f_n1.after(G.g))
                if G.tail:
                    sp.dma_start(out[GROUPS * GB * P:N, :], x1[0:LAST, GROUPS * GB, :]).then_inc(f_o, 16)
                else:
                    sp.dma_start(out_groups[:, bass.ds(G.g * GB, GB), :], x1[:, bass.ds(G.g * GB, GB), :]).then_inc(f_o, 16)
            groups(sp, store)
            sp.wait_ge(f_o, 16 * (GROUPS + 1))

        @block.gpsimd
        def _(pool):
            nc.gpsimd.memset(ident[:, :], 0.0).then_inc(s_const, 1)
            pool.wait_ge(s_const, 1)
            nc.gpsimd.affine_select(out=ident[:, :], in_=ident[:, :], compare_op=ALU.not_equal, fill=1.0,
                                    base=0, pattern=[[-1, P]], channel_multiplier=1).then_inc(s_const, 1)
            nc.gpsimd.iota(node_iota[:, :], [[1, P]], base=0, channel_multiplier=0,
                           allow_small_or_imprecise_dtypes=True).then_inc(s_const, 1)
            nc.gpsimd.memset(ones[:, :], 1.0).then_inc(s_const, 1)
            nc.gpsimd.iota(pass_tab[0:1, 0, 1:PASSES], [[1, BLOCKS]], base=QUADS, channel_multiplier=0).then_inc(s_const, 1)
            nc.gpsimd.memset(pass_tab[0:1, 0, 0:1], 0).then_inc(s_const, 1)
            nc.gpsimd.memset(pass_tab[0:1, 1, 1:PASSES], 0).then_inc(s_const, 1)
            nc.gpsimd.memset(pass_tab[0:1, 1, 0:1], 1).then_inc(s_const, 1)
            nc.gpsimd.iota(moved[:, :], [[P, PASSES]], base=0, channel_multiplier=0,
                           allow_small_or_imprecise_dtypes=True).then_inc(s_const, 1)
            nc.gpsimd.iota(win_tab[0:1, QUADS:QUADS + BLOCKS], [[2, BLOCKS]], base=0, channel_multiplier=0).then_inc(s_const, 1)
            nc.gpsimd.iota(pair_tab[0:1, 0:PAIRS], [[2, PAIRS]], base=0, channel_multiplier=0).then_inc(s_const, 1)
            nc.gpsimd.memset(pair_tab[0:1, PAIRS:], PAIRS * 2 - 2).then_inc(s_const, 1)
            nc.gpsimd.memset(cnt[:, :], 0.0).then_inc(s_clear, 1)
            pool.wait_ge(s_etr, 4)
            nc.gpsimd.memset(agg[:, :], 0.0).then_inc(s_clear, 1)

            def write_source_part(G):
                pool.wait_ge(ac.sem, ac.after(G.g))
                pool.sem_inc(gm, 1)
                if G.tail:
                    pool.dma_start(src_rows[GROUPS * GB * P:, :], a_out[:, 0, 0, :]).then_inc(aw[0], 16)
                else:
                    pool.dma_start(src_groups[:, bass.ds(G.g * GB, GB), :], a_out[:, G.b, :, :]).then_inc(aw[G.b], 16)

            def split_target_part(G):
                pool.wait_ge(rests.sem, rests.after(G.g))
                pool.sem_inc(gm, 1)
                nc.gpsimd.tensor_tensor(third_of(G, 2), bres[:, G.b, 0:G.nb, :], third_of(G, 1), ALU.subtract).then_inc(thirds.sem, 1)
            start_credits(pool, thirds)
            skewed(pool, write_source_part, split_target_part)

            def gather(k, table):
                l = L[k]
                used = l["used"]
                passes = pool.value_load(passes_i[0:1, 0:1], min_val=1, max_val=PASSES)
                with pool.Fori(0, passes) as p:
                    with pool.Fori(0, ITERS) as i:
                        n0 = pool.snap((p * ITERS + i) * SLOTS)
                        h0 = pool.snap((p * ITERS + i) * 2)
                        for s in range(SLOTS):
                            if s % HALF == 0:
                                pool.wait_ge(l["staged"], h0 + (s // HALF + 1))
                            pool.wait_ge(used.sem, used.after(n0 + (s - SLOTS)))
                            pool.sem_inc(l["issued"], 1)
                            for j in range(QT):
                                c = (s % HALF) * QT + j
                                nc.gpsimd.indirect_dma_start(
                                    rows[:, s, j, :], None, table,
                                    bass.IndirectOffsetOnAxis(ap=idx_stage[:, s // HALF, c:c + 1], axis=0),
                                ).then_inc(l["gathered"][s], 16)

            pool.wait_ge(s_tab, 1)
            pool.wait_ge(aw[0], 16 * (GROUPS // 2 + 1))
            pool.wait_ge(aw[1], 16 * (GROUPS // 2))
            pool.wait_ge(s_tupc, 1)
            gather(0, src_rows)

            def keep_x1(G):
                pool.wait_ge(u_x1.sem, u_x1.after(G.g))
                pool.sem_inc(gm, 1)
                if G.tail:
                    nc.gpsimd.tensor_copy(x1[:, GROUPS * GB, :], x1s[:, 0, 0, :]).then_inc(u_x1k.sem, 1)
                else:
                    nc.gpsimd.tensor_copy(x1[:, bass.ds(G.g * GB, GB), :], x1s[:, G.b, :, :]).then_inc(u_x1k.sem, 1)
            groups(pool, keep_x1)
            for k in range(GB):
                pool.wait_ge(u_hw[k], 16 * (GROUPS + (k == 0)))
            gather(1, rel_rows)

            def cap_z(G):
                b, nb = G.b, G.nb
                pool.wait_ge(f_z.sem, f_z.after(G.g))
                pool.wait_ge(f_t.sem, f_t.after(G.g - 2))
                pool.sem_inc(gm, 1)
                nc.gpsimd.tensor_scalar(cap[:, b, 0:nb, :], zb[:, b, 0:nb, :], EXP_CAP, None, ALU.min).then_inc(f_cap.sem, 1)

            def products(G):
                b, nb = G.b, G.nb
                pool.wait_ge(f_r.sem, f_r.after(G.g))
                nc.gpsimd.tensor_tensor(ez[:, b, 0:nb, :], ez[:, b, 0:nb, :], cap[:, b, 0:nb, :], ALU.mult).then_inc(f_t.sem, 1)
                pool.wait_ge(f_t.sem, f_t.after(G.g))
                pool.wait_ge(f_tr.sem, f_tr.after(G.g - 2))
                nc.gpsimd.tensor_tensor(mish_out[:, b, 0:nb, :], zb[:, b, 0:nb, :], ez[:, b, 0:nb, :], ALU.mult).then_inc(f_m.sem, 1)
            start_credits(pool, f_cap, f_t, f_m)
            skewed(pool, cap_z, products)

        @block.tensor
        def _(pe):
            pe.wait_ge(s_const, 10)
            pe.wait_ge(s_cast, 3)
            for k in range(4):
                for c in range(CH):
                    t = rawf[:, k, c, :] if k < 3 else raw_w[:, c, :]
                    ins = nc.tensor.transpose(bank[2 * k + c // 4][:, (c % 4) * P:(c % 4 + 1) * P], t, ident[:, :])
                ins.then_inc(s_etr, 1)
            start_credits(pe, xtr, abm, p_tr, p_mm, u_mm, u_t1, u_root, u_h0, u_h1, f_tr)
            for l in L:
                start_credits(pe, l["onehot_turned"], l["looked_up"], l["scattered"])
            pe.wait_ge(s_ecp, 8)
            pe.wait_ge(s_wab, 16)

            def prepare_turn(G):
                if G.tail:
                    pe.wait_ge(s_xtail, 16)
                else:
                    pe.wait_ge(xl[G.b], G.pair * 16 + 16)
                pe.wait_ge(xtc.sem, xtc.after(G.g - 2))
                for k in range(G.nb):
                    ins = nc.tensor.transpose(bank[G.b][:, k * P:(k + 1) * P], x_block(G, k), ident[:, :])
                ins.then_inc(xtr.sem, 1)

            def prepare(G):
                pe.wait_ge(xtc.sem, xtc.after(G.g))
                pe.wait_ge(ac.sem, ac.after(G.g - 2))
                pe.wait_ge(bc.sem, bc.after(G.g - 2))
                if G.first and G.b == 1:
                    pe.wait_ge(s_nfar, 1)
                    nc.tensor.matmul(bank[3][0:1, 0:1], n_far[:, :], ones[:, 0:1], start=True, stop=True).then_inc(s_nfars, 1)
                    pe.wait_ge(s_tab, 1)
                for part in range(2):
                    for k in range(G.nb):
                        ins = nc.tensor.matmul(bank[2 + 2 * part + G.b][:, k * P:(k + 1) * P], xT[:, G.b, k, :],
                                               w_ab[:, part, :], start=True, stop=True)
                ins.then_inc(abm.sem, 1)
                if G.first and G.b == 0:
                    pe.wait_ge(s_base, 1)
                    nc.tensor.matmul(bank[5][:, 0:QUADS], ones[0:1, :], win_f, start=True, stop=True).then_inc(s_baseb, 1)
                if G.tail:
                    pe.wait_ge(s_wup, 32)
                    nc.tensor.matmul(bank[6][:, 0:P], xT[:, 0, 0, :], w_up[:, 0, :], start=True, stop=True)
                    nc.tensor.matmul(bank[6][:, P:2 * P], xT[:, 0, 0, :], w_self[:, :], start=True, stop=True).then_inc(s_tup, 1)
            skewed(pe, prepare_turn, prepare)

            def edge_loop(k):
                l = L[k]
                passes = pe.value_load(passes_i[0:1, 0:1], min_val=1, max_val=PASSES)
                with pe.Fori(0, passes) as p:
                    at, step = pass_values(pe, p)
                    with pe.Fori(0, ITERS) as i:
                        it = pe.snap(p * ITERS + i)
                        n0 = pe.snap(it * SLOTS)

                        def turn(s):
                            b, n = s % 2, n0 + s
                            pe.wait_ge(l["onehot_ready"].sem, l["onehot_ready"].after(n))
                            pe.wait_ge(l["turned_copied"].sem, l["turned_copied"].after(n - 2))
                            for j in range(QT):
                                ins = nc.tensor.transpose(bank[b][:, j * P:(j + 1) * P], onehot[:, s % 4, j, :], ident[:, :])
                            ins.then_inc(l["onehot_turned"].sem, 1)

                        def look_up(s):
                            b, n = s % 2, n0 + s
                            w = window_of(pe, i, s, at, step)
                            pe.wait_ge(l["turned_copied"].sem, l["turned_copied"].after(n))
                            pe.wait_ge(l["lookup_used"].sem, l["lookup_used"].after(n - 2))
                            if k == 0:
                                table = tgt_win.rearrange("p q h k c -> p (q h) (k c)")
                                for j in range(QT):
                                    for h in range(3):
                                        ins = nc.tensor.matmul(
                                            bank[2 + b][:, j * P:(j + 1) * P], onehot_t[:, b, j, :],
                                            table[:, bass.ds(w, 1), h * C:(h + 1) * C],
                                            start=(h == 0), stop=(h == 2))
                            else:
                                table = inv_win[:, :, :, :, :].rearrange("p q h k r -> p (q h) (k r)")
                                for j in range(QT):
                                    ins = nc.tensor.matmul(bank[2 + b][:, j * 3 * R:(j + 1) * 3 * R], onehot_t[:, b, j, :],
                                                           table[:, bass.ds(w, 1), :], start=True, stop=True)
                            ins.then_inc(l["looked_up"].sem, 1)

                        def scatter(s):
                            b, n = s % 2, n0 + s
                            pe.wait_ge(l["messages_ready"].sem, l["messages_ready"].after(n))
                            pe.wait_ge(l["window_added"].sem, l["window_added"].after(n - 2))
                            if k == 0:
                                pe.wait_ge(l["counts_added"].sem, l["counts_added"].after(n - 2))
                            for j in range(QT):
                                ins = nc.tensor.matmul(bank[4 + b][:, 0:P], msg[:, b, j, :], onehot[:, s % 4, j, :],
                                                       start=(j == 0), stop=(j == QT - 1))
                            if k == 0:
                                for j in range(QT):
                                    ins = nc.tensor.matmul(bank[4 + b][:, P:P + R], onehot[:, s % 4, j, :], types[:, s % 4, j, :],
                                                           start=(j == 0), stop=(j == QT - 1))
                            ins.then_inc(l["scattered"].sem, 1)

                        def turn_pair():
                            pe.wait_ge(p_l, (it + 1) * 16)
                            pe.wait_ge(p_tc.sem, p_tc.after(it - 1))
                            for j in range(2):
                                ins = nc.tensor.transpose(bank[6][:, j * P:(j + 1) * P], pair_x[:, j, :], ident[:, :])
                            ins.then_inc(p_tr.sem, 1)

                        def multiply_pair():
                            pe.wait_ge(p_tc.sem, p_tc.after(it))
                            pe.wait_ge(p_c.sem, p_c.after(it - 1))
                            for j in range(2):
                                for u, w in enumerate((w_up[:, 0, :], w_self[:, :])):
                                    ins = nc.tensor.matmul(bank[7][:, (j * 2 + u) * P:(j * 2 + u + 1) * P], pair_xT[:, j, :], w,
                                                           start=True, stop=True)
                            ins.then_inc(p_mm.sem, 1)

                        turn(0)
                        for s in range(SLOTS):
                            if s + 1 < SLOTS:
                                turn(s + 1)
                            look_up(s)
                            if s >= 1:
                                scatter(s - 1)
                            if k == 0 and s == 1:
                                turn_pair()
                            if k == 0 and s == HALF:
                                multiply_pair()
                        scatter(SLOTS - 1)

            pe.wait_ge(ac.sem, ac.after(GROUPS))
            pe.wait_ge(bc.sem, bc.after(GROUPS))
            pe.wait_ge(s_tupc, 1)
            pe.wait_ge(s_odd, 32)
            pe.wait_ge(s_tab, 1)
            pe.wait_ge(s_w2, 16 * 7)
            edge_loop(0)

            pe.wait_ge(l_done[0], 1)

            def update(G):
                pe.wait_ge(u_st.sem, u_st.after(G.g))
                pe.wait_ge(u_y.sem, u_y.after(G.g - 1))
                for k in range(G.nb):
                    ins = nc.tensor.matmul(bank[3][:, k * P:(k + 1) * P], aT[:, G.b, k, :], w_up[:, 1, :], start=True, stop=True)
                ins.then_inc(u_mm.sem, 1)

            def relations(G):
                pe.wait_ge(u_x1.sem, u_x1.after(G.g))
                pe.wait_ge(u_t1c.sem, u_t1c.after(G.g - 1))
                for k in range(G.nb):
                    ins = nc.tensor.transpose(bank[4][:, k * P:(k + 1) * P], x1s[:, G.b, k, :], ident[:, :])
                ins.then_inc(u_t1.sem, 1)
                if not G.tail:
                    update(Group(G.pair, G.b + 1))
                pe.wait_ge(u_t1c.sem, u_t1c.after(G.g))
                pe.wait_ge(u_rootc.sem, u_rootc.after(G.g - 1))
                nc.tensor.matmul(bank[5][:, 0:G.nb * P], w_ro[:, :], x1T[:, 0:G.nb, :], start=True, stop=True).then_inc(u_root.sem, 1)
                for k in range(G.nb):
                    n = G.g * GB + k
                    for h, (done, copied) in enumerate(((u_h0, u_hc0), (u_h1, u_hc1))):
                        pe.wait_ge(copied.sem, copied.after(n - 1))
                        nc.tensor.matmul(bank[6 + h][:, :], x1T[:, k, :], w_r[:, h * (R // 2):(h + 1) * (R // 2), :],
                                         start=True, stop=True).then_inc(done.sem, 1)
            update(Group(0, 0))
            groups(pe, relations)

            pe.wait_ge(u_rootc.sem, u_rootc.after(GROUPS))
            pe.wait_ge(u_hc0.sem, u_hc0.after(GROUPS * GB))
            pe.wait_ge(u_hc1.sem, u_hc1.after(GROUPS * GB))
            pe.wait_ge(c_upd, (GROUPS + 1) * UPD_STEPS)
            pe.wait_ge(s_oddi, 32)
            edge_loop(1)

            def turn_back(G):
                b, nb = G.b, G.nb
                pe.wait_ge(f_y.sem, f_y.after(G.g - 2))
                nc.tensor.matmul(bank[b][:, 0:nb * P], ident[:, :], x1[:, bass.ds(G.g * GB, nb), :], start=True, stop=False)
                pe.wait_ge(f_m.sem, f_m.after(G.g))
                for k in range(nb):
                    ins = nc.tensor.matmul(bank[b][:, k * P:(k + 1) * P], mish_out[:, b, k, :], ident[:, :], start=False, stop=(k == nb - 1))
                ins.then_inc(f_tr.sem, 1)
            pe.wait_ge(l_done[1], 1)
            groups(pe, turn_back)

        @block.scalar
        def _(act):
            for k, d in enumerate((src_f, dst_f, type_f, dist)):
                act.wait_ge(s_etr, k + 1)
                nc.scalar.copy(d[:, 0:512], bank[2 * k][:, :]).then_inc(s_ecp, 1)
                nc.scalar.copy(d[:, 512:COLS], bank[2 * k + 1][:, 0:COLS - 512]).then_inc(s_ecp, 1)
            start_credits(act, xtc, ac, p_tc, p_c, u_sd, u_t1c, u_rootc, u_hc0, u_hc1, f_z, f_exp, f_d, f_y, f_n1, L[1]["used"])
            for l in L:
                start_credits(act, l["turned_copied"], l["messages_ready"])

            def prepare_turn(G):
                b, nb = G.b, G.nb
                act.wait_ge(xtr.sem, xtr.after(G.g))
                act.wait_ge(abm.sem, abm.after(G.g - 2))
                nc.scalar.copy(xT[:, b, 0:nb, :], bank[b][:, 0:nb * P].rearrange("p (k c) -> p k c", c=C)).then_inc(xtc.sem, 1)

            def prepare(G):
                b, nb = G.b, G.nb
                if not G.first:
                    act.wait_ge(aw[b], G.pair * 16)
                act.wait_ge(abm.sem, abm.after(G.g))
                nc.scalar.copy(a_out[:, b, 0:nb, :], bank[2 + b][:, 0:nb * P].rearrange("p (k c) -> p k c", c=C)).then_inc(ac.sem, 1)
                if G.tail:
                    act.wait_ge(s_tup, 1)
                    nc.scalar.copy(upd_out[:, 0, :, :], bank[6][:, 0:2 * P].rearrange("p (u c) -> p u c", u=2)).then_inc(s_tupc, 1)
            skewed(act, prepare_turn, prepare)

            def edge_loop(k):
                l = L[k]
                passes = act.value_load(passes_i[0:1, 0:1], min_val=1, max_val=PASSES)
                with act.Fori(0, passes) as p:
                    with act.Fori(0, ITERS) as i:
                        it = act.snap(p * ITERS + i)
                        n0 = act.snap(it * SLOTS)

                        def copy_turned(s):
                            b, n = s % 2, n0 + s
                            act.wait_ge(l["onehot_turned"].sem, l["onehot_turned"].after(n))
                            act.wait_ge(l["looked_up"].sem, l["looked_up"].after(n - 2))
                            nc.scalar.copy(onehot_t[:, b, :, :], bank[b][:, :].rearrange("p (k c) -> p k c", c=P)
                                           ).then_inc(l["turned_copied"].sem, 1)

                        def message(s):
                            b, n = s % 2, n0 + s
                            act.wait_ge(l["scattered"].sem, l["scattered"].after(n - 2))
                            act.wait_ge(l["lookup_used"].sem, l["lookup_used"].after(n))
                            if k == 0:
                                nc.scalar.activation(msg[:, b, :, :], pre[:, b, :, :], ACT.Relu).then_inc(l["messages_ready"].sem, 1)
                            else:
                                act.wait_ge(l["gathered"][s], (it + 1) * (16 * QT))
                                for j in range(QT):
                                    ins = nc.scalar.activation(msg[:, b, j, :], rows[:, s, j, :], ACT.Copy,
                                                               scale=edge_w[:, b, j:j + 1])
                                ins.then_inc(l["messages_ready"].sem, 1)
                                act.wait_ge(l["messages_ready"].sem, l["messages_ready"].after(n))
                                act.sem_inc(l["used"].sem, 1)

                        def copy_pair():
                            act.wait_ge(p_tr.sem, p_tr.after(it))
                            act.wait_ge(p_mm.sem, p_mm.after(it - 1))
                            nc.scalar.copy(pair_xT, bank[6][:, 0:2 * P].rearrange("p (k c) -> p k c", k=2)).then_inc(p_tc.sem, 1)

                        def copy_products():
                            act.wait_ge(p_w, (it + 1) * 16)
                            act.wait_ge(p_mm.sem, p_mm.after(it))
                            nc.scalar.copy(upd_out, bank[7][:, :].rearrange("p (k u c) -> p k u c", k=2, u=2)).then_inc(p_c.sem, 1)

                        copy_turned(0)
                        for s in range(SLOTS):
                            if s + 1 < SLOTS:
                                copy_turned(s + 1)
                            message(s)
                            if k == 0 and s == 2:
                                copy_pair()
                            if k == 0 and s == HALF + 1:
                                copy_products()
            edge_loop(0)

            def relations(G):
                nb = G.nb
                act.wait_ge(u_t1.sem, u_t1.after(G.g))
                act.wait_ge(u_h1.sem, u_h1.after(G.g * GB - 1))
                nc.scalar.copy(x1T[:, 0:nb, :], bank[4][:, 0:nb * P].rearrange("p (k c) -> p k c", c=C)).then_inc(u_t1c.sem, 1)
                act.wait_ge(u_root.sem, u_root.after(G.g))
                act.sem_inc(gm, 1)
                nc.scalar.activation(agg[:, bass.ds(G.g * (GB * P), nb * P)], bank[5][:, 0:nb * P], ACT.Identity,
                                     bias=chan[:, 0:1]).then_inc(u_rootc.sem, 1)
                for k in range(nb):
                    if k == nb - 2:
                        deviation(Group(G.pair, G.b + 1))
                    if not (isinstance(G.g, int) and G.g == 0):
                        act.wait_ge(u_hw[k], G.g * 16)
                    act.wait_ge(u_h0.sem, u_h0.after(G.g * GB + k))
                    nc.scalar.copy(hs[:, k, 0:R * C // 2], bank[6][:, :]).then_inc(u_hc0.sem, 1)
                    act.wait_ge(u_h1.sem, u_h1.after(G.g * GB + k))
                    nc.scalar.copy(hs[:, k, R * C // 2:], bank[7][:, :]).then_inc(u_hc1.sem, 1)

            def deviation(G):
                act.wait_ge(u_var.sem, u_var.after(G.g))
                nc.scalar.activation(sd[:, 0:G.nb], vare[:, 0:G.nb], ACT.Sqrt).then_inc(u_sd.sem, 1)

            deviation(Group(0, 0))
            groups(act, relations)
            edge_loop(1)

            act.wait_ge(s_bv, 1)
            nc.scalar.activation(baff[:, 1:2], baff[:, 0:1], ACT.Sqrt).then_inc(s_bsd, 1)
            act.wait_ge(s_aff, 1)

            def exponential(G):
                b, nb = G.b, G.nb
                act.wait_ge(f_m.sem, f_m.after(G.g - 2))
                act.sem_inc(gm, 1)
                nc.scalar.activation(zb[:, b, 0:nb, :], agg[:, bass.ds(G.g * (GB * P), nb * P)].rearrange("p (k c) -> p k c", c=P),
                                     ACT.Identity, bias=baff[:, 4:5], scale=baff[:, 3:4]).then_inc(f_z.sem, 1)
                act.wait_ge(f_cap.sem, f_cap.after(G.g))
                nc.scalar.activation(ez[:, b, 0:nb, :], cap[:, b, 0:nb, :], ACT.Exp).then_inc(f_exp.sem, 1)
                if G.first:
                    divisor(G)

            def divisor(G):
                b, nb = G.b, G.nb
                act.wait_ge(f_u.sem, f_u.after(G.g))
                nc.scalar.activation(cap[:, b, 0:nb, :], ez[:, b, 0:nb, :], ACT.Copy, bias=2.0).then_inc(f_d.sem, 1)

            def keep_rows(G):
                act.wait_ge(f_tr.sem, f_tr.after(G.g))
                act.sem_inc(gm, 1)
                nc.scalar.copy(x1[:, bass.ds(G.g * GB, G.nb), :], bank[G.b][:, 0:G.nb * P].rearrange("p (k c) -> p k c", c=C)
                               ).then_inc(f_y.sem, 1)
                if not G.beyond:
                    divisor(Group(G.pair, G.b + 2))
            skewed(act, exponential, keep_rows, 2)
            nc.scalar.activation(sd[:, 0:1], vare[:, 0:1], ACT.Sqrt)
            act.wait_ge(s_fv, 1)
            nc.scalar.activation(sdall[:, 1, :], sdall[:, 0, :], ACT.Sqrt).then_inc(s_fsd, 1)
            act.wait_ge(s_scale, 1)

            def normalise(G):
                if G.tail:
                    return
                for k in range(1, GB, 2):
                    n = G.g * GB + k
                    ins = nc.scalar.activation(x1[:, bass.ds(n, 1), :], x1[:, bass.ds(n, 1), :], ACT.Identity,
                                               bias=sdall[:, 0, bass.ds(n, 1)], scale=sdall[:, 2, bass.ds(n, 1)])
                ins.then_inc(f_n1.sem, 1)
            groups(act, normalise)

        @block.vector
        def _(dve):
            v = nc.vector
            start_credits(dve, bc, rests, u_st, u_y, u_var, u_x1, u_x1k, f_u, f_r, f_n)
            start_credits(dve, L[0]["used"])
            for l in L:
                start_credits(dve, *(l[s] for s in ("onehot_ready", "lookup_used", "picked_ready", "window_added", "counts_added")))
            for k, pad in enumerate((0, FAR, 0)):
                v.memset(raw[:, k, CH - 1, :], pad).then_inc(s_pad, 1)
            v.memset(raw_w[:, CH - 1, :], 0.0).then_inc(s_pad, 1)
            v.memset(x_tail[LAST // 32 * 32:, :], 0.0).then_inc(s_tail, 1)
            v.memset(cnt_odd[0:P // 2, 0, :], 0.0).then_inc(s_clear, 1)
            v.memset(inv_win[P // 2:P, BLOCKS - 1, 1, :, :], 0.0).then_inc(s_clear, 1)
            v.memset(tgt_win[P // 2:P, BLOCKS - 1, 1, :, :], 0.0).then_inc(s_clear, 1)
            dve.wait_ge(s_edges, 16 * 12)
            for k in range(3):
                v.tensor_copy(rawf[:, k, :, :], raw[:, k, :, :]).then_inc(s_cast, 1)
            dve.wait_ge(s_ecp, 8)
            ch = Chain(dve, c_edge)
            for o, n in ((0, TILES), (TILES, BODY_T)):
                ch.step(v.tensor_copy(idx[0][:, o:o + n], src_f[:, 0:n]))
            ch.step(v.tensor_copy(first_i, dst_f[0:1, 0:TILES:QT]))
            ch.step(v.tensor_scalar(win_tab[0:1, 0:QUADS], first_i, 6, None, ALU.arith_shift_right))
            v.tensor_scalar(win_f, win_tab[0:1, 0:QUADS], 64.0, None, ALU.mult).then_inc(s_base, 1)
            dve.wait_ge(s_baseb, 1)
            ch.step(v.tensor_tensor(rel0[:, :].rearrange("p (q j) -> p q j", j=QT),
                                    dst_f[:, 0:TILES].rearrange("p (q j) -> p q j", j=QT),
                                    bank[5][:, 0:QUADS].unsqueeze(2).broadcast_to([P, QUADS, QT]), ALU.subtract))
            ch.step(v.tensor_scalar(outside[:, :], rel0[:, :], 0.0, None, ALU.is_ge))
            ch.step(v.scalar_tensor_tensor(out=inside, in0=rel0[:, :], scalar=float(P), in1=outside[:, :],
                                           op0=ALU.is_lt, op1=ALU.mult))
            ch.step(v.scalar_tensor_tensor(out=outside[:, :], in0=dst_f[:, 0:TILES], scalar=float(FAR // 2), in1=inside,
                                           op0=ALU.is_lt, op1=ALU.subtract))
            v.reduce_sum(n_far[:, :], outside[:, :], AX.X).then_inc(s_nfar, 1)
            dve.wait_ge(s_nfars, 1)
            ch.step(v.tensor_scalar(passes_f[:, 0:1], bank[3][0:1, 0:1], 1.0, float(BLOCKS), ALU.min, ALU.mult))
            v.tensor_scalar(passes_i[:, :], passes_f[:, 0:1], 1.0, None, ALU.add).then_inc(s_tab, 1)
            dve.wait_ge(s_bm, 16)

            def stage_first(k):
                v.tensor_copy(idx_stage[:, :, :], idx[k][:, 0:BODY_T].rearrange("p (h c) -> p h c", h=2)).then_inc(L[k]["staged"], 2)

            stage_first(0)

            def prepare(G):
                nb = G.nb
                ch = Chain(dve, c_prep, G.g * PREP_STEPS)
                dve.wait_ge(abm.sem, abm.after(G.g))
                part, rest = bsum[:, 0:nb, :], bres[:, G.b, 0:nb, :]
                ch.step(v.tensor_tensor(part, bank[4 + G.b][:, 0:nb * P].rearrange("p (k c) -> p k c", c=C), over(bmsg, nb), ALU.add))
                dve.sem_inc(bc.sem, 1)
                ch.step(v.tensor_copy(third_of(G, 0), part))
                dve.wait_ge(thirds.sem, thirds.after(G.g - 2))
                dve.sem_inc(gm, 1)
                ch.step(v.tensor_tensor(rest, part, third_of(G, 0), ALU.subtract))
                ch.step(v.tensor_copy(third_of(G, 1), rest))
                dve.sem_inc(rests.sem, 1)
            groups(dve, prepare)
            ch = Chain(dve, c_far)
            ch.step(v.scalar_tensor_tensor(out=far0[:, :], in0=dst_f[:, 0:TILES], scalar=float(FAR), in1=outside[:, :],
                                           op0=ALU.add, op1=ALU.mult))
            ch.step(v.tensor_scalar(far0[:, :], far0[:, :], float(-FAR), None, ALU.add))
            dve.wait_ge(s_w2, 16 * 7)

            def edge_loop(k):
                l = L[k]
                v.tensor_copy(rel[:, :], rel0[:, :]).then_inc(l["targets"], 1)
                passes = dve.value_load(passes_i[0:1, 0:1], min_val=1, max_val=PASSES)
                with dve.Fori(0, passes) as p:
                    at, step = pass_values(dve, p)
                    dve.wait_ge(l["targets"], p + 1)
                    dve.sem_inc(gm, 1)
                    with dve.Fori(0, ITERS) as i:
                        it = dve.snap(p * ITERS + i)
                        n0 = dve.snap(it * SLOTS)

                        def one_hot(s):
                            b, n = s % 4, n0 + s
                            col = i * BODY_T + s * QT
                            dve.wait_ge(l["scattered"].sem, l["scattered"].after(n - 4))
                            for j in range(QT):
                                v.tensor_scalar(onehot[:, b, j, :], node_iota[:, :], rel[:, bass.ds(col + j, 1)], None, ALU.is_equal)
                            ins = v.tensor_tensor(
                                types[:, b, :, :], node_iota[:, 0:R].unsqueeze(1).broadcast_to([P, QT, R]),
                                type_f[:, bass.ds(col, QT)].unsqueeze(2).broadcast_to([P, QT, R]), ALU.is_equal)
                            ins.then_inc(l["onehot_ready"].sem, 1)

                        def weigh(s):
                            b, n = s % 2, n0 + s
                            dve.wait_ge(l["messages_ready"].sem, l["messages_ready"].after(n - 2))
                            dve.wait_ge(l["gathered"][s], (it + 1) * (16 * QT))
                            for j in range(QT):
                                ins = v.scalar_tensor_tensor(
                                    out=pre[:, b, j, :], in0=w_dist[:, :], scalar=dist[:, bass.ds(i * BODY_T + (s * QT + j), 1)],
                                    in1=rows[:, s, j, :], op0=ALU.mult, op1=ALU.add)
                            ins.then_inc(l["used"].sem, 1)

                        def use_lookup(s):
                            b, n = s % 2, n0 + s
                            dve.wait_ge(l["looked_up"].sem, l["looked_up"].after(n))
                            if k == 0:
                                dve.wait_ge(l["used"].sem, l["used"].after(n))
                                v.tensor_tensor(pre[:, b, :, :], pre[:, b, :, :], bank[2 + b][:, :].rearrange("p (k c) -> p k c", c=C),
                                                ALU.add).then_inc(l["lookup_used"].sem, 1)
                            else:
                                dve.wait_ge(l["messages_ready"].sem, l["messages_ready"].after(n - 2))
                                dve.wait_ge(l["lookup_used"].sem, l["lookup_used"].after(n - 1))
                                v.tensor_tensor(picked[:, :, :, :], bank[2 + b][:, 0:QT * 3 * R].rearrange("p (j h r) -> p j h r", j=QT, h=3),
                                                types[:, s % 4, :, :].unsqueeze(2).broadcast_to([P, QT, 3, R]), ALU.mult
                                                ).then_inc(l["picked_ready"].sem, 1)
                                dve.wait_ge(l["picked_ready"].sem, l["picked_ready"].after(n))
                                v.reduce_sum(edge_w[:, b, :], picked[:, :, :, :].rearrange("p j h r -> p j (h r)"), AX.X).then_inc(l["lookup_used"].sem, 1)

                        def add_window(s):
                            b, n = s % 2, n0 + s
                            w = window_of(dve, i, s, at, step)
                            node = dve.snap(w * (P // 2))
                            dve.wait_ge(l["scattered"].sem, l["scattered"].after(n))
                            dve.wait_ge(l["window_added"].sem, l["window_added"].after(n - 1))
                            v.tensor_tensor(agg[:, bass.ds(node, P)], agg[:, bass.ds(node, P)], bank[4 + b][:, 0:P], ALU.add
                                            ).then_inc(l["window_added"].sem, 1)
                            if k == 0:
                                dve.wait_ge(l["counts_added"].sem, l["counts_added"].after(n - 1))
                                v.tensor_tensor(cnt[:, bass.ds(w, 1), :], cnt[:, bass.ds(w, 1), :], bank[4 + b][:, P:P + R].unsqueeze(1), ALU.add
                                                ).then_inc(l["counts_added"].sem, 1)

                        def restage(h):
                            dve.wait_ge(l["messages_ready"].sem, l["messages_ready"].after(n0 + (h * HALF + HALF - 1)))
                            v.tensor_scalar(idx_stage[:, h, :], idx[k][:, bass.ds(i * BODY_T + (h * STAGE_T + BODY_T), STAGE_T)],
                                            0.0, None, ALU.add).then_inc(l["staged"], 1)

                        one_hot(0)
                        one_hot(1)
                        for s in range(SLOTS):
                            if k == 0:
                                weigh(s)
                            if s + 2 < SLOTS:
                                one_hot(s + 2)
                            use_lookup(s)
                            if s >= 1:
                                add_window(s - 1)
                            if s == HALF:
                                restage(0)
                        add_window(SLOTS - 1)
                        restage(1)
                    dve.wait_ge(l["onehot_ready"].sem, l["onehot_ready"].after((p + 1) * QUADS - 1))
                    v.tensor_scalar(rel[:, :], far0[:, :], moved[:, bass.ds(p, 1)], None, ALU.subtract).then_inc(l["targets"], 1)
                end = passes * QUADS - 1
                dve.wait_ge(l["window_added"].sem, l["window_added"].after(end))
                if k == 0:
                    dve.wait_ge(l["counts_added"].sem, l["counts_added"].after(end))
                dve.sem_inc(l_done[k], 1)

            dve.wait_ge(s_clear, 5)
            dve.wait_ge(thirds.sem, thirds.after(GROUPS))
            edge_loop(0)

            def norm_statistics(ch, values, nb):
                for k in range(nb):
                    ins = v.bn_stats(st6[:, k, :], values(k))
                ch.step(ins)
                dve.sem_inc(gm, 1)
                for k in range(nb):
                    ins = v.bn_aggr(mv[:, k, :], st6[:, k, :])
                ch.step(ins)

            def stage_sums(G):
                b, nb = G.b, G.nb
                dve.wait_ge(u_mm.sem, u_mm.after(G.g - 2))
                v.tensor_scalar(aT[:, b, 0:nb, :], agg[:, bass.ds(G.g * (GB * P), nb * P)].rearrange("p (k c) -> p k c", c=P),
                                1.0, None, ALU.mult).then_inc(u_st.sem, 1)

            def update(G):
                b, nb = G.b, G.nb
                ch = Chain(dve, c_upd, G.g * UPD_STEPS)
                dve.wait_ge(u_mm.sem, u_mm.after(G.g))
                dve.wait_ge(url[b], G.pair * 16 + 16)
                if not G.tail:
                    dve.wait_ge(ul[b], G.pair * 16 + 16)
                yy, y1 = y[:, 0:nb, :], y2[:, 0:nb, :]
                ch.step(v.tensor_tensor(y1, bank[3][:, 0:nb * P].rearrange("p (k c) -> p k c", c=C), upd_in[:, b, 0:nb, 0, :], ALU.add))
                ch.step(v.tensor_tensor(y1, y1, over(bupd, nb), ALU.add))
                ch.step(v.scalar_tensor_tensor(out=yy, in0=y1, scalar=0.0, in1=upd_in[:, b, 0:nb, 1, :], op0=ALU.max, op1=ALU.add))
                ch.step(v.tensor_tensor(yy, yy, x_tail[:, :].unsqueeze(1) if G.tail else xs[:, b, 0:nb, :], ALU.add))
                dve.sem_inc(u_y.sem, 1)
                norm_statistics(ch, lambda k: y[:, k, :], nb)
                v.tensor_scalar(vare[:, 0:nb], mv[:, 0:nb, 1], EPS, None, ALU.add).then_inc(u_var.sem, 1)
                dve.wait_ge(u_sd.sem, u_sd.after(G.g))
                ch.step(v.reciprocal(rstd[:, 0:nb], sd[:, 0:nb]))
                dve.wait_ge(u_x1k.sem, u_x1k.after(G.g - 2))
                dve.wait_ge(u_t1.sem, u_t1.after(G.g - 2))
                for k in range(nb):
                    ins = v.tensor_scalar(x1s[:, b, k, :], y[:, k, :], mv[:, k, 0:1], rstd[:, k:k + 1], ALU.subtract, ALU.mult)
                ch.step(ins)
                dve.sem_inc(u_x1.sem, 1)

            skewed(dve, stage_sums, update)
            ch = Chain(dve, c_idx)
            for o, n in ((0, TILES), (TILES, BODY_T)):
                ch.step(v.scalar_tensor_tensor(out=idx[1][:, o:o + n], in0=idx[0][:, 0:n], scalar=float(R),
                                               in1=type_f[:, 0:n], op0=ALU.mult, op1=ALU.add))
            stage_first(1)

            ch = Chain(dve, c_inv)
            dve.wait_ge(s_oddc, 32)
            even = cnt[:, :, :].rearrange("p (q h) r -> p q h r", h=2)[:, :, 0, :]
            ch.step(v.tensor_tensor(inv[:, :, :], even, cnt_odd[:, :, :], ALU.add))
            ch.step(v.tensor_scalar(cnt_odd[:, :, :], inv[:, :, :], 1.0, None, ALU.max))
            ch.step(v.reciprocal(inv[:, :, :], cnt_odd[:, :, :]))
            ch.step(v.tensor_copy(inv3[:, :, 0, :], inv[:, :, :]))
            ch.step(v.tensor_tensor(cnt_odd[:, :, :], inv[:, :, :], inv3[:, :, 0, :], ALU.subtract))
            ch.step(v.tensor_copy(inv3[:, :, 1, :], cnt_odd[:, :, :]))
            v.tensor_tensor(inv3[:, :, 2, :], cnt_odd[:, :, :], inv3[:, :, 1, :], ALU.subtract).then_inc(s_inv, 1)

            dve.wait_ge(u_rootc.sem, u_rootc.after(GROUPS))
            dve.wait_ge(u_x1k.sem, u_x1k.after(GROUPS))
            edge_loop(1)

            ch = Chain(dve, c_fin)
            for c in range(NST):
                ins = v.bn_stats(bst[:, c, :], agg[:, c * SC:(c + 1) * SC])
            ch.step(ins)
            ch.step(v.bn_aggr(bmv[:, :], bst[:, :, :].rearrange("p a b -> p (a b)")))
            v.tensor_scalar(baff[:, 0:1], bmv[:, 1:2], EPS, None, ALU.add).then_inc(s_bv, 1)
            dve.wait_ge(s_bsd, 1)
            ch.step(v.reciprocal(baff[:, 2:3], baff[:, 1:2]))
            ch.step(v.tensor_tensor(baff[:, 3:4], baff[:, 2:3], chan[:, 1:2], ALU.mult))
            ch.step(v.tensor_tensor(baff[:, 5:6], bmv[:, 0:1], baff[:, 3:4], ALU.mult))
            v.tensor_tensor(baff[:, 4:5], chan[:, 2:3], baff[:, 5:6], ALU.subtract).then_inc(s_aff, 1)
            start = ch.n

            def numerator(G):
                e = ez[:, G.b, 0:G.nb, :]
                dve.wait_ge(f_exp.sem, f_exp.after(G.g))
                v.scalar_tensor_tensor(out=e, in0=e, scalar=2.0, in1=e, op0=ALU.add, op1=ALU.mult).then_inc(f_u.sem, 1)
                if G.first:
                    invert(G)

            def invert(G):
                c = cap[:, G.b, 0:G.nb, :]
                dve.wait_ge(f_d.sem, f_d.after(G.g))
                v.reciprocal(c, c).then_inc(f_r.sem, 1)

            def row_statistics(G):
                ch = Chain(dve, c_fin, G.g * 3 + start)
                dve.wait_ge(f_y.sem, f_y.after(G.g))
                dve.sem_inc(gm, 1)
                norm_statistics(ch, lambda k: x1[:, bass.ds(G.g * GB + k, 1), :], G.nb)
                ch.step(v.tensor_scalar(mvall[:, bass.ds(G.g * GB, G.nb), :], mv[:, 0:G.nb, :], 1.0, None, ALU.mult))
                if not G.beyond:
                    invert(Group(G.pair, G.b + 2))
            skewed(dve, numerator, row_statistics, 2)
            v.tensor_scalar(sdall[:, 0, :], mvall[:, :, 1], EPS, None, ALU.add).then_inc(s_fv, 1)
            dve.wait_ge(s_fsd, 1)
            ch = Chain(dve, c_nrm)
            ch.step(v.reciprocal(sdall[:, 2, :], sdall[:, 1, :]))

            ch.step(v.scalar_tensor_tensor(out=sdall[:, 0, :], in0=mvall[:, :, 0], scalar=-1.0, in1=sdall[:, 2, :],
                                           op0=ALU.mult, op1=ALU.mult))
            dve.sem_inc(s_scale, 1)

            def normalise(G):
                for k in range(0, G.nb, 2):
                    n = G.g * GB + k
                    ins = v.tensor_scalar(x1[:, bass.ds(n, 1), :], x1[:, bass.ds(n, 1), :], mvall[:, bass.ds(n, 1), 0],
                                          sdall[:, 2, bass.ds(n, 1)], ALU.subtract, ALU.mult)
                ins.then_inc(f_n.sem, 1)
            groups(dve, normalise)


_INS = ["x", "src", "dst", "edge_type_8", "edge_weight1", "L0_gnn_W_res", "L0_gnn_W_msg", "L0_gnn_b_msg", "L0_gnn_W_upd",
        "L0_gnn_b_upd", "L1_gnn_W", "L1_gnn_root", "L1_gnn_bias", "L1_gnn_gamma", "L1_gnn_beta"]


def kernel(**inputs):
    import numpy as _np
    import concourse.bacc as _bacc
    from concourse import mybir as _mybir
    from concourse.bass_utils import run_bass_kernel_spmd as _run

    nc = _bacc.Bacc("TRN2", target_bir_lowering=False, num_devices=1)
    arrays, args = {}, []
    for name in _INS:
        a = _np.ascontiguousarray(inputs[name])
        arrays[f"in_{name}_dram"] = a
        args.append(nc.dram_tensor(f"in_{name}_dram", a.shape, _mybir.dt.from_np(a.dtype), kind="ExternalInput").ap())
    args.append(nc.dram_tensor("out_0_dram", inputs["x"].shape, _mybir.dt.float32, kind="ExternalOutput").ap())
    bass_gnn(nc, *args)
    r = _run(nc, [arrays], core_ids=[0])
    return r.results[0]["out_0_dram"]
```
